# Optimizing a Trainium2 kernel written in Bass

```python
import numpy as np
import jax
import jax.numpy as jnp

def _softmax(x, axis=-1):
    return jax.nn.softmax(x, axis=axis)

def _gelu(x):
    return jax.nn.gelu(x, approximate=True)

def _silu(x):
    return jax.nn.silu(x)

def _sigmoid(x):
    return jax.nn.sigmoid(x)

def _layernorm(x, axis=-1, eps=1e-05):
    m = jnp.mean(x, axis=axis, keepdims=True)
    v = jnp.var(x, axis=axis, keepdims=True)
    return (x - m) / jnp.sqrt(v + eps)

def _scatter_add(tgt, idx, src, axis=0):
    return tgt.at[idx].add(src)

def _segment_sum(src, seg, n):
    return jax.ops.segment_sum(src, seg, n)
kernel_name = 'mk_cond_seq_d2_seqx_r4_638fbe'

def setup_inputs(seed: int=0):
    np.random.seed(seed)
    _w = jnp.asarray

    def _rec_inputs():
        import jax
        import jax.numpy as jnp
        _rk = jax.random.key(seed)
        x = -0.0005207 + 1.001 * jax.random.normal(jax.random.fold_in(_rk, 1), (4, 512, 256), jnp.float32)
        _lenS = 512 - jax.random.randint(jax.random.fold_in(_rk, 7), (4,), 0, max(1, 512 // 4) + 1, jnp.int32)
        _lenS2 = 512 - jax.random.randint(jax.random.fold_in(_rk, 8), (4,), 0, max(1, 512 // 4) + 1, jnp.int32)
        itok_B_34_63 = jax.random.randint(jax.random.fold_in(_rk, 12), (4,), 34, 64, jnp.int32)
        fside_Bx16xSxS_0 = -1.47943e-05 + 1.00017 * jax.random.normal(jax.random.fold_in(_rk, 13), (4, 16, 512, 512), jnp.float32)
        condB_gatescore = jax.random.uniform(jax.random.fold_in(_rk, 14), (4,), jnp.float32, 0.0, 0.581427)
        _validS = jnp.arange(512)[None, :] < _lenS[:, None]
        _validS2 = jnp.arange(512)[None, :] < _lenS2[:, None]
        _causal = jnp.tril(jnp.ones((512, 512), dtype=bool))
        mask_Bx1xSxS_bk0 = jnp.logical_not(jnp.broadcast_to(_validS[:, None, None, :], (4, 1, 512, 512)))
        return (x, itok_B_34_63, fside_Bx16xSxS_0, condB_gatescore, mask_Bx1xSxS_bk0)
    x, itok_B_34_63, fside_Bx16xSxS_0, condB_gatescore, mask_Bx1xSxS_bk0 = _rec_inputs()

    def _L0_cond_setup():
        import jax, jax.numpy as jnp
        import numpy as np
        import math
        D_MODEL = 256
        N_HEAD = 16
        HEAD_DIM = D_MODEL // N_HEAD
        D_FF = 1024
        NUM_STEPS = 100.0
        RESCALE = 4000.0
        EPS = 1e-05

        def _sin_emb(t):
            half = D_MODEL // 2
            x = t.astype(jnp.float32) / NUM_STEPS * RESCALE
            freqs = jnp.exp(jnp.arange(half, dtype=jnp.float32) * (-math.log(10000.0) / (half - 1)))
            e = x[:, None] * freqs[None, :]
            return jnp.concatenate([jnp.sin(e), jnp.cos(e)], axis=-1)

        def _ln(x):
            m = jnp.mean(x, axis=-1, keepdims=True)
            v = jnp.var(x, axis=-1, keepdims=True)
            return (x - m) / jnp.sqrt(v + EPS)

        def _gelu2(x):
            return x * jax.nn.sigmoid(1.702 * x)
        key = jax.random.key(seed)
        ks = jax.random.split(key, 24)
        B, S, D, F = (4, 128, D_MODEL, D_FF)
        std = 0.02
        inp = {'src': jax.random.normal(ks[0], (B, S, D), dtype=jnp.float32), 'src_mask': jax.random.randint(ks[1], (B, 1, S, S), 0, 2).astype(bool), 'timestep': jax.random.randint(ks[2], (B,), 0, 100, dtype=jnp.int32), 'attention_bias': jax.random.normal(ks[3], (B, N_HEAD, S, S), dtype=jnp.float32), 'W_ada': jax.random.normal(ks[4], (D, 2 * D), dtype=jnp.float32) * std, 'b_ada': jnp.zeros((2 * D,), dtype=jnp.float32), 'Wq': jax.random.normal(ks[5], (D, D), dtype=jnp.float32) * std, 'bq': jnp.zeros((D,), dtype=jnp.float32), 'Wk': jax.random.normal(ks[6], (D, D), dtype=jnp.float32) * std, 'bk': jnp.zeros((D,), dtype=jnp.float32), 'Wv': jax.random.normal(ks[7], (D, D), dtype=jnp.float32) * std, 'bv': jnp.zeros((D,), dtype=jnp.float32), 'Wo': jax.random.normal(ks[8], (D, D), dtype=jnp.float32) * std, 'bo': jnp.zeros((D,), dtype=jnp.float32), 'W1': jax.random.normal(ks[9], (D, F), dtype=jnp.float32) * std, 'b1': jnp.zeros((F,), dtype=jnp.float32), 'W2': jax.random.normal(ks[10], (F, D), dtype=jnp.float32) * std, 'b2': jnp.zeros((D,), dtype=jnp.float32), 'g2': jnp.ones((D,), dtype=jnp.float32), 'beta2': jnp.zeros((D,), dtype=jnp.float32)}
        return inp
    _L0_cond_all = _L0_cond_setup()
    _L0_cond_in = {k: v for k, v in _L0_cond_all.items() if k in ('W_ada', 'b_ada', 'Wq', 'bq', 'Wk', 'bk', 'Wv', 'bv', 'Wo', 'bo', 'W1', 'b1', 'W2', 'b2', 'g2', 'beta2')}
    del _L0_cond_all

    def _L1_cond_setup():
        import jax, jax.numpy as jnp
        import numpy as np
        D_MODEL = 256
        N_HEADS = 16
        D_HEAD = D_MODEL // N_HEADS
        D_FF = 1024
        EPS = 1e-05

        def layernorm(x, gamma, beta):
            mu = jnp.mean(x, axis=-1, keepdims=True)
            var = jnp.var(x, axis=-1, keepdims=True)
            return (x - mu) * jax.lax.rsqrt(var + EPS) * gamma + beta
        key = jax.random.key(seed)
        ks = jax.random.split(key, 16)
        B, T = (4, 512)
        s = 1.0 / np.sqrt(D_MODEL)
        sf = 1.0 / np.sqrt(D_FF)
        return {'x': jax.random.normal(ks[0], (B, T, D_MODEL), jnp.float32), 'gate_score': jax.random.uniform(ks[1], (B,), jnp.float32), 'Wq': jax.random.normal(ks[2], (D_MODEL, D_MODEL), jnp.float32) * s, 'bq': jnp.zeros((D_MODEL,), jnp.float32), 'Wk': jax.random.normal(ks[3], (D_MODEL, D_MODEL), jnp.float32) * s, 'bk': jnp.zeros((D_MODEL,), jnp.float32), 'Wv': jax.random.normal(ks[4], (D_MODEL, D_MODEL), jnp.float32) * s, 'bv': jnp.zeros((D_MODEL,), jnp.float32), 'Wo': jax.random.normal(ks[5], (D_MODEL, D_MODEL), jnp.float32) * s, 'bo': jnp.zeros((D_MODEL,), jnp.float32), 'W1': jax.random.normal(ks[6], (D_MODEL, D_FF), jnp.float32) * s, 'b1': jnp.zeros((D_FF,), jnp.float32), 'W2': jax.random.normal(ks[7], (D_FF, D_MODEL), jnp.float32) * sf, 'b2': jnp.zeros((D_MODEL,), jnp.float32), 'gamma1': jnp.ones((D_MODEL,), jnp.float32), 'beta1': jnp.zeros((D_MODEL,), jnp.float32), 'gamma2': jnp.ones((D_MODEL,), jnp.float32), 'beta2': jnp.zeros((D_MODEL,), jnp.float32)}
    _L1_cond_all = _L1_cond_setup()
    _L1_cond_in = {k: v for k, v in _L1_cond_all.items() if k in ('Wq', 'bq', 'Wk', 'bk', 'Wv', 'bv', 'Wo', 'bo', 'W1', 'b1', 'W2', 'b2', 'gamma1', 'beta1', 'gamma2', 'beta2')}
    del _L1_cond_all
    return {'x': x, 'itok_B_34_63': itok_B_34_63, 'fside_Bx16xSxS_0': fside_Bx16xSxS_0, 'condB_gatescore': condB_gatescore, 'mask_Bx1xSxS_bk0': mask_Bx1xSxS_bk0, 'L0_cond_W_ada': _L0_cond_in['W_ada'], 'L0_cond_b_ada': _L0_cond_in['b_ada'], 'L0_cond_Wq': _L0_cond_in['Wq'], 'L0_cond_bq': _L0_cond_in['bq'], 'L0_cond_Wk': _L0_cond_in['Wk'], 'L0_cond_bk': _L0_cond_in['bk'], 'L0_cond_Wv': _L0_cond_in['Wv'], 'L0_cond_bv': _L0_cond_in['bv'], 'L0_cond_Wo': _L0_cond_in['Wo'], 'L0_cond_bo': _L0_cond_in['bo'], 'L0_cond_W1': _L0_cond_in['W1'], 'L0_cond_b1': _L0_cond_in['b1'], 'L0_cond_W2': _L0_cond_in['W2'], 'L0_cond_b2': _L0_cond_in['b2'], 'L0_cond_g2': _L0_cond_in['g2'], 'L0_cond_beta2': _L0_cond_in['beta2'], 'L1_cond_Wq': _L1_cond_in['Wq'], 'L1_cond_bq': _L1_cond_in['bq'], 'L1_cond_Wk': _L1_cond_in['Wk'], 'L1_cond_bk': _L1_cond_in['bk'], 'L1_cond_Wv': _L1_cond_in['Wv'], 'L1_cond_bv': _L1_cond_in['bv'], 'L1_cond_Wo': _L1_cond_in['Wo'], 'L1_cond_bo': _L1_cond_in['bo'], 'L1_cond_W1': _L1_cond_in['W1'], 'L1_cond_b1': _L1_cond_in['b1'], 'L1_cond_W2': _L1_cond_in['W2'], 'L1_cond_b2': _L1_cond_in['b2'], 'L1_cond_gamma1': _L1_cond_in['gamma1'], 'L1_cond_beta1': _L1_cond_in['beta1'], 'L1_cond_gamma2': _L1_cond_in['gamma2'], 'L1_cond_beta2': _L1_cond_in['beta2']}

def reference(x, itok_B_34_63, fside_Bx16xSxS_0, condB_gatescore, mask_Bx1xSxS_bk0, L0_cond_W_ada, L0_cond_b_ada, L0_cond_Wq, L0_cond_bq, L0_cond_Wk, L0_cond_bk, L0_cond_Wv, L0_cond_bv, L0_cond_Wo, L0_cond_bo, L0_cond_W1, L0_cond_b1, L0_cond_W2, L0_cond_b2, L0_cond_g2, L0_cond_beta2, L1_cond_Wq, L1_cond_bq, L1_cond_Wk, L1_cond_bk, L1_cond_Wv, L1_cond_bv, L1_cond_Wo, L1_cond_bo, L1_cond_W1, L1_cond_b1, L1_cond_W2, L1_cond_b2, L1_cond_gamma1, L1_cond_beta1, L1_cond_gamma2, L1_cond_beta2):
    import jax
    import jax.numpy as jnp

    def _L0_cond_ref(src, src_mask, timestep, attention_bias, W_ada, b_ada, Wq, bq, Wk, bk, Wv, bv, Wo, bo, W1, b1, W2, b2, g2, beta2):
        import jax, jax.numpy as jnp
        import numpy as np
        import math
        D_MODEL = 256
        N_HEAD = 16
        HEAD_DIM = D_MODEL // N_HEAD
        D_FF = 1024
        NUM_STEPS = 100.0
        RESCALE = 4000.0
        EPS = 1e-05

        def _sin_emb(t):
            half = D_MODEL // 2
            x = t.astype(jnp.float32) / NUM_STEPS * RESCALE
            freqs = jnp.exp(jnp.arange(half, dtype=jnp.float32) * (-math.log(10000.0) / (half - 1)))
            e = x[:, None] * freqs[None, :]
            return jnp.concatenate([jnp.sin(e), jnp.cos(e)], axis=-1)

        def _ln(x):
            m = jnp.mean(x, axis=-1, keepdims=True)
            v = jnp.var(x, axis=-1, keepdims=True)
            return (x - m) / jnp.sqrt(v + EPS)

        def _gelu2(x):
            return x * jax.nn.sigmoid(1.702 * x)
        B, S, D = src.shape
        emb = jax.nn.silu(_sin_emb(timestep)) @ W_ada + b_ada
        scale, shift = jnp.split(emb[:, None, :], 2, axis=-1)
        x = _ln(src) * (1.0 + scale) + shift
        q = (x @ Wq + bq).reshape(B, S, N_HEAD, HEAD_DIM).transpose(0, 2, 1, 3)
        k = (x @ Wk + bk).reshape(B, S, N_HEAD, HEAD_DIM).transpose(0, 2, 1, 3)
        v = (x @ Wv + bv).reshape(B, S, N_HEAD, HEAD_DIM).transpose(0, 2, 1, 3)
        scores = jnp.einsum('bhqd,bhkd->bhqk', q / math.sqrt(HEAD_DIM), k)
        scores = scores + attention_bias
        scores = jnp.where(src_mask, -jnp.inf, scores.astype(jnp.float32))
        probs = jax.nn.softmax(scores, axis=-1).astype(v.dtype)
        ctx = jnp.einsum('bhqk,bhkd->bhqd', probs, v)
        ctx = ctx.transpose(0, 2, 1, 3).reshape(B, S, D)
        x = x + (ctx @ Wo + bo)
        h = _ln(x) * g2 + beta2
        ff = _gelu2(h @ W1 + b1) @ W2 + b2
        return x + ff

    def _L1_cond_ref(x, gate_score, Wq, bq, Wk, bk, Wv, bv, Wo, bo, W1, b1, W2, b2, gamma1, beta1, gamma2, beta2):
        import jax, jax.numpy as jnp
        import numpy as np
        D_MODEL = 256
        N_HEADS = 16
        D_HEAD = D_MODEL // N_HEADS
        D_FF = 1024
        EPS = 1e-05

        def layernorm(x, gamma, beta):
            mu = jnp.mean(x, axis=-1, keepdims=True)
            var = jnp.var(x, axis=-1, keepdims=True)
            return (x - mu) * jax.lax.rsqrt(var + EPS) * gamma + beta
        B, T, C = x.shape
        h = layernorm(x, gamma1, beta1)
        Q = (h @ Wq + bq).reshape(B, T, N_HEADS, D_HEAD).transpose(0, 2, 1, 3)
        K = (h @ Wk + bk).reshape(B, T, N_HEADS, D_HEAD).transpose(0, 2, 1, 3)
        V = (h @ Wv + bv).reshape(B, T, N_HEADS, D_HEAD).transpose(0, 2, 1, 3)
        scores = jnp.einsum('bhqd,bhkd->bhqk', Q, K) / np.sqrt(D_HEAD)
        causal = jnp.tril(jnp.ones((T, T), dtype=bool))
        scores = jnp.where(causal, scores, -jnp.inf)
        attn = jax.nn.softmax(scores, axis=-1)
        ctx = jnp.einsum('bhqk,bhkd->bhqd', attn, V)
        ctx = ctx.transpose(0, 2, 1, 3).reshape(B, T, C)
        attn_out = ctx @ Wo + bo
        x1 = x + attn_out
        h2 = layernorm(x1, gamma2, beta2)
        ff = jax.nn.gelu(h2 @ W1 + b1, approximate=False) @ W2 + b2
        x2 = x1 + ff
        g = gate_score[:, None, None]
        return x + g * (x2 - x)
    x = _L0_cond_ref(x, mask_Bx1xSxS_bk0, itok_B_34_63, fside_Bx16xSxS_0, L0_cond_W_ada, L0_cond_b_ada, L0_cond_Wq, L0_cond_bq, L0_cond_Wk, L0_cond_bk, L0_cond_Wv, L0_cond_bv, L0_cond_Wo, L0_cond_bo, L0_cond_W1, L0_cond_b1, L0_cond_W2, L0_cond_b2, L0_cond_g2, L0_cond_beta2)
    x = _L1_cond_ref(x, condB_gatescore, L1_cond_Wq, L1_cond_bq, L1_cond_Wk, L1_cond_bk, L1_cond_Wv, L1_cond_bv, L1_cond_Wo, L1_cond_bo, L1_cond_W1, L1_cond_b1, L1_cond_W2, L1_cond_b2, L1_cond_gamma1, L1_cond_beta1, L1_cond_gamma2, L1_cond_beta2)
    return x

_drawn_inputs = setup_inputs


def setup_inputs(seed=0):
    import zlib

    import numpy as np

    out = dict(_drawn_inputs(seed))
    spreads = {'L0_cond_b_ada': (0.0, 0.1),
     'L0_cond_bq': (0.0, 0.8),
     'L0_cond_bk': (0.0, 2.0),
     'L0_cond_bv': (0.0, 0.275),
     'L0_cond_bo': (0.0, 0.1),
     'L0_cond_b1': (0.0, 0.1),
     'L0_cond_b2': (0.0, 0.1),
     'L0_cond_g2': (1.0, 0.6),
     'L0_cond_beta2': (0.0, 0.768),
     'L1_cond_bq': (0.0, 0.8),
     'L1_cond_bk': (0.0, 2.0),
     'L1_cond_bv': (0.0, 0.355),
     'L1_cond_bo': (0.0, 0.383),
     'L1_cond_b1': (0.0, 0.648),
     'L1_cond_b2': (0.0, 0.462),
     'L1_cond_gamma1': (1.0, 0.6),
     'L1_cond_beta1': (0.0, 0.334),
     'L1_cond_gamma2': (1.0, 0.58),
     'L1_cond_beta2': (0.0, 0.63)}
    factors = {'fside_Bx16xSxS_0': 8.0, 'L0_cond_Wq': 8.0, 'L0_cond_Wk': 8.0, 'L0_cond_Wv': 3.067}
    for name, (base, spread) in spreads.items():
        noise = np.random.default_rng([zlib.crc32(name.encode()), seed]).standard_normal(out[name].shape)
        drawn = base * np.exp(spread * noise) if base else spread * noise
        out[name] = jnp.asarray(drawn.astype(out[name].dtype))
    for name, factor in factors.items():
        out[name] = (out[name] * factor).astype(out[name].dtype)
    return out
```

```python
from contextlib import ExitStack

import numpy as np

import concourse.bass as bass
from concourse import mybir

F32 = mybir.dt.float32
BF16 = mybir.dt.bfloat16
U8 = mybir.dt.uint8
I32 = mybir.dt.int32
ALU = mybir.AluOpType
ACT = mybir.ActivationFunctionType
AX_X = mybir.AxisListType.X

P = 128
B, S, D = 4, 512, 256
H, DH, F = 16, 16, 1024
T = S // P
C = D // P
FC = F // P
G = 4
NG = H // G
QW = 32
PARTS = 3
Q_ROLE = [0, 0, 1, 0, 2, 1]
K_ROLE = [0, 1, 0, 2, 0, 1]
ROWS = DH * len(Q_ROLE)
SHIFT = ROWS + PARTS
QSCALE = DH ** -0.5
EPS = 1e-5
BIG = 1e37
GELU_K = 1.702
NUM_STEPS, RESCALE = 100.0, 4000.0
ROUND = 12582912.0
TWO_PI_HI, TWO_PI_MID = 6.28125, 0.0019350051879882812
TWO_PI_LO = float(2 * np.pi - TWO_PI_HI - TWO_PI_MID)
PI_IN = 3.1415925

FREE = 1

T1, QK, VV, OO, T2, F1, F2 = 0, 2, 6, 10, 14, 16, 24
FILLS = 28


def width(t):
    return (t + 1) * P


def drainer(layer, d):
    if d < VV or T2 <= d < F1:
        return "a"
    if F1 <= d < F2:
        return "a" if layer else "v"
    return "v"


def drains(layer, d):
    return sum(drainer(layer, e) == drainer(layer, d) for e in range(d + 1))


DRAINS = [{e: sum(drainer(l, d) == e for d in range(FILLS)) for e in "av"} for l in range(2)]
V_STEPS = [27, 28]


def two_layers(nc, a, out):
    freqs = np.exp(np.arange(P, dtype=np.float32) * np.float32(-np.log(10000.0) / (P - 1)))
    freq_table = nc.inline_tensor(freqs.astype(np.float32).reshape(P, 1))
    freq_dram = freq_table.ap()
    part_dram = nc.dram_tensor("part_dram", (2, PARTS, D, S), BF16, kind="Internal").ap()
    max_dram = nc.dram_tensor("max_dram", (NG, PARTS * G * T, P), BF16, kind="Internal").ap()
    bias_dram = a["fside_Bx16xSxS_0"].rearrange("b h (t p) k -> (b h) p t k", p=P)
    x_dram = a["x"].rearrange("b (t p) d -> b p t d", p=P)
    out_dram = out.rearrange("b (t p) d -> b p t d", p=P)
    mask_dram = a["mask_Bx1xSxS_bk0"].rearrange("b o (t p) k -> (b o) p t k", p=P)
    par = [{k.removeprefix(f"L{l}_cond_"): v for k, v in a.items() if k.startswith(f"L{l}_")} for l in range(2)]
    gam = [par[0]["g2"], par[1]["gamma2"]]
    bet = [par[0]["beta2"], par[1]["beta2"]]

    nc.disable_value_cache = True

    with ExitStack() as ctx:
        def sb(name, shape, dt=F32):
            return ctx.enter_context(nc.sbuf_tensor(name, shape, dt))

        def ps(name, shape, dt=F32):
            return ctx.enter_context(nc.psum_tensor(name, shape, dt))

        def sem(name):
            return ctx.enter_context(nc.semaphore(name))

        def sem2(name):
            return [sem(f"{name}{l}") for l in range(2)]

        wq, wk, wv, wo = ([sb(f"{n}{l}", [P, C, D]) for l in range(2)] for n in ("wq", "wk", "wv", "wo"))
        w1 = [sb(f"w1_{l}", [P, C, F]) for l in range(2)]
        w2 = [sb(f"w2_{l}", [P, FC, D]) for l in range(2)]
        bqk = [sb(f"bqk{l}", [P, 2, C]) for l in range(2)]
        b1 = [sb(f"b1_{l}", [P, FC]) for l in range(2)]
        b1k = sb("b1k", [P, FC])
        gb1 = sb("gb1", [P, 2, C])
        gb2 = [sb(f"gb2_{l}", [P, 2, C]) for l in range(2)]
        bv_all = [sb(f"bv_all{l}", [P, D]) for l in range(2)]
        bo_all = [sb(f"bo_all{l}", [P, D]) for l in range(2)]
        b2_all = [sb(f"b2_all{l}", [P, D]) for l in range(2)]
        gate = sb("gate", [P, B, 1])
        ada = sb("ada", [P, B, 2 * D])
        ident = sb("ident", [P, P])
        ident_b = sb("ident_b", [P, P], BF16)
        later_key = sb("later_key", [P, P], BF16)
        later_key_t = sb("later_key_t", [P, P], BF16)
        free = sb("free", [P, 32])
        freq = sb("freq", [P, 1])
        step_i = sb("step_i", [P, B], I32)
        emb = sb("emb", [P, 8, 2, B])
        mask_u8 = sb("mask_u8", [P, T, S], U8)
        mask_neg = sb("mask_neg", [P, T, S])
        mask_row = sb("mask_row", [P, 3, T])
        xin, xh, xr, resb, x1, xl1 = (sb(n, [P, T, D]) for n in ("xin", "xh", "xr", "resb", "x1", "xl1"))
        yout = xr
        stats = sb("stats", [P, T, 6])
        mv = sb("mv", [P, T, 2])
        var_eps, rstd, neg_half = (sb(n, [P, T]) for n in ("var_eps", "rstd", "neg_half"))
        hT = sb("hT", [P, C, S])
        q6 = sb("q6", [P, H, S], BF16)
        k6 = sb("k6", [P, H, S], BF16)
        vx = sb("vx", [P, T, H, QW])
        bias = sb("bias", [P, G, T, S])
        rmax = sb("rmax", [P, H, T])
        rneg = sb("rneg", [P, 2, 2, G * T])
        mparts = sb("mparts", [P, 2, PARTS, G * T], BF16)
        mT = sb("mT", [PARTS * G * T, 2, P], BF16)
        sums = x1[:, 0:2, :].rearrange("p t n -> p (t n)")
        ctxn = hT
        ctxd = xh[:, :, :].rearrange("p (c a) n -> p c (a n)", c=C)
        work = sb("work", [P, G * T * S])
        prob = work[:, :].rearrange("p (g n) -> p g n", g=G)
        qkf = work[:, 0:2048].rearrange("p (x c n) -> p x c n", x=2, c=C)
        rem = work[:, 2048:4096].rearrange("p (x c n) -> p x c n", x=2, c=C)
        part = work[:, 4096:7168].bitcast(BF16).rearrange("p (x w c n) -> p x w c n", x=2, w=PARTS, c=C)
        gT = work[:, 0:4096].rearrange("p (f n) -> p f n", f=FC)
        sig = work[:, 4096:5120].rearrange("p (i n) -> p i n", i=2)
        wada = work[:, 0:1024].rearrange("p (c n) -> p c n", c=C)
        bada = work[:, 1024:1536]
        act_bc = work[:, 2048:3072].rearrange("p (c b n) -> p c b n", c=C, b=B)

        psS = ps("psS", [P, 2, S])
        psT = ps("psT", [P, 4, S])
        psC = ps("psC", [P, S])
        psM = ps("psM", [P, 1024], BF16)

        weights_in, ada_w_in, consts_in = sem("weights_in"), sem("ada_w_in"), sem("consts_in")
        made = sem("made")
        embed, embed_act, ada_filled, ada_ready = (sem(n) for n in ("embed", "embed_act", "ada_filled", "ada_ready"))
        small_ready = sem("small_ready")
        x_in, mask_in, mask_ready, xin_used = sem("x_in"), sem("mask_in"), sem("mask_ready"), sem("xin_used")
        bias_in = [sem(f"bias_in{s}") for s in range(G)]
        bias_masked, scores_subbed = sem("bias_masked"), sem("scores_subbed")
        v_step, measured = sem2("v_step"), sem2("measured")
        stats_ready, rstd_ready, norm_ready = sem2("stats_ready"), sem2("rstd_ready"), sem2("norm_ready")
        res_ready = sem2("res_ready")
        filled, drained_a, drained_v = sem2("filled"), sem2("drained_a"), sem2("drained_v")
        parts_ready, parts_out, roles_in = sem2("parts_ready"), sem2("parts_out"), sem2("roles_in")
        s_filled, s_drained = sem2("s_filled"), sem2("s_drained")
        t_filled, exped = sem2("t_filled"), sem2("exped")
        pv_done, ctx_drained = sem2("pv_done"), sem2("ctx_drained")
        compacted = [[sem(f"compacted{l}_{g}") for g in range(2)] for l in range(2)]
        mparts_ready, m_filled, m_drained = sem("mparts_ready"), sem("m_filled"), sem("m_drained")
        m_out = sem("m_out")
        m_rows = [sem(f"m_rows{g}") for g in range(2)]
        sig_ready = sem("sig_ready")
        y_ready, y_out = sem("y_ready"), sem("y_out")

        N_W, N_C, N_MADE, N_EMBED, N_SMALL = 16 * 12, 16 * 19, 9, 15, 5 + B

        def wait_drained(eng, l, b, d):
            e = drainer(l, d)
            if e == "a":
                eng.wait_ge(drained_a[l], b * DRAINS[l][e] + drains(l, d))
            else:
                eng.wait_ge(drained_v[l], FREE + b * DRAINS[l][e] + drains(l, d))

        class Target:

            def __init__(self, eng, sem, first, step):
                self.eng, self.sem, self.step = eng, sem, step
                self.reg = eng.alloc_register()
                eng.reg_mov(self.reg, first)

            def wait(self):
                self.eng.wait_ge(self.sem, self.reg)
                self.eng.reg_add(self.reg, self.reg, self.step)

        block = ctx.enter_context(nc.Block())

        @block.sync
        def _(sp):
            def col(v, n):
                return v.rearrange("(c p) -> p c", p=P)[:, 0:n]

            def row_all(v, n):
                return v.rearrange("(a n) -> a n", a=1).to_broadcast([P, n])

            sp.dma_start(wada, par[0]["W_ada"].rearrange("(c p) n -> p c n", p=P)).then_inc(ada_w_in, 16)
            sp.dma_start(bada, row_all(par[0]["b_ada"], 2 * D)).then_inc(ada_w_in, 16)
            sp.dma_start(step_i[:, :], a["itok_B_34_63"].rearrange("(a n) -> a n", a=1).to_broadcast([P, B])).then_inc(ada_w_in, 16)
            sp.dma_start(freq[:, :], freq_dram).then_inc(ada_w_in, 16)
            sp.dma_start(gate[:, :, 0], row_all(a["condB_gatescore"], B)).then_inc(consts_in, 16)
            n = 16
            for l in range(2):
                loads = [(bqk[l][:, 0, :], col(par[l]["bq"], C)), (bqk[l][:, 1, :], col(par[l]["bk"], C)),
                         (b1[l][:, :], col(par[l]["b1"], FC)), (gb2[l][:, 0, :], col(gam[l], C)),
                         (gb2[l][:, 1, :], col(bet[l], C)), (bv_all[l][:, :], row_all(par[l]["bv"], D)),
                         (bo_all[l][:, :], row_all(par[l]["bo"], D)), (b2_all[l][:, :], row_all(par[l]["b2"], D))]
                if l:
                    loads += [(gb1[:, 0, :], col(par[1]["gamma1"], C)), (gb1[:, 1, :], col(par[1]["beta1"], C))]
                for dst, src in loads:
                    with nc.allow_non_contiguous_dma(reason="per-channel columns, once"):
                        sp.dma_start(dst, src).then_inc(consts_in, 16)
                    n += 16
            assert n == N_C
            n = 0
            for l in range(2):
                for dst, name in ((wq, "Wq"), (wk, "Wk"), (wv, "Wv"), (wo, "Wo"), (w1, "W1"), (w2, "W2")):
                    sp.dma_start(dst[l][:, :, :], par[l][name].rearrange("(c p) n -> p c n", p=P)).then_inc(weights_in, 16)
                    n += 16
            assert n == N_W

            def to_roles(l, b):
                for x in range(2):
                    if l:
                        sp.wait_ge(roles_in[0], FREE + (b + 1) * 192)
                    else:
                        sp.wait_ge(roles_in[1], FREE + b * 192)
                    sp.wait_ge(parts_ready[l], b * 2 + x + 1)
                    sp.dma_start(part_dram[x].rearrange("w (c p) n -> p w c n", p=P), part[:, x, :, :, :]).then_inc(parts_out[l], 16)
                if l:
                    sp.wait_ge(pv_done[0], FREE + (b + 1) * NG * T)
                else:
                    sp.wait_ge(pv_done[1], FREE + b * NG * T)
                sp.wait_ge(parts_out[l], b * 32 + 32)
                for x, (dst, roles) in enumerate(((q6, Q_ROLE), (k6, K_ROLE))):
                    for r, w in enumerate(roles):
                        sp.dma_start(dst[r * DH:(r + 1) * DH, :, :],
                                     part_dram[x, w].rearrange("(h d) n -> d h n", d=DH)).then_inc(roles_in[l], 16)

            def compact(l, b, g):
                sp.wait_ge(ctx_drained[l], FREE + b * NG + g + 1)
                for j in range(G):
                    at = (g % 2) * G * DH + j * DH
                    sp.dma_start(ctxd[at:at + DH, g // 2, :], ctxn[j * QW:j * QW + DH, g % 2, :]).then_inc(compacted[l][g % 2], 16)

            def max_rows(b, g):
                sp.wait_ge(m_drained, FREE + b * NG + g + 1)
                sp.dma_start(max_dram[g], mT[:, g % 2, :]).then_inc(m_out, 16)
                sp.wait_ge(m_out, b * 16 * NG + 16 * (g + 1))
                sp.dma_start(q6[ROWS:SHIFT, g * G:(g + 1) * G, :].rearrange("p h (t k) -> p (h t) k", k=P),
                             max_dram[g].rearrange("(w r) k -> w r k", w=PARTS)).then_inc(m_rows[g % 2], 16)

            with sp.Fori(0, B) as b:
                sp.wait_ge(mask_ready, FREE + b)
                sp.dma_start(xin[:, :, :], x_dram[b]).then_inc(x_in, 16)
                sp.dma_start(mask_u8[:, :, :], mask_dram[b]).then_inc(mask_in, 16)
                for h in range(G):
                    sp.wait_ge(t_filled[0], FREE + b * 2 * H)
                    sp.dma_start(bias[:, h, :, :], bias_dram[b * H + h]).then_inc(bias_in[h], 16)
                to_roles(0, b)
                for h in range(G, H):
                    sp.wait_ge(t_filled[0], FREE + b * 2 * H + 2 * (h - G) + 2)
                    sp.dma_start(bias[:, h % G, :, :], bias_dram[b * H + h]).then_inc(bias_in[h % G], 16)
                    if h >= 2 * G + 2 and h % G == 2:
                        compact(0, b, h // G - 2)
                compact(0, b, NG - 2)
                compact(0, b, NG - 1)
                to_roles(1, b)
                for g in range(NG):
                    max_rows(b, g)
                    if g >= 3:
                        compact(1, b, g - 3)
                for g in range(1, NG):
                    compact(1, b, g)

        @block.gpsimd
        def _(pool):
            from_free = [xin_used, mask_ready, m_drained, m_filled, y_out, bias_masked, *t_filled, *roles_in, *pv_done,
                         *drained_v, *s_drained, *ctx_drained, *compacted[0], *compacted[1]]
            for i, s in enumerate(from_free):
                pool.memset(free[:, i:i + 1], 0.0).then_inc(s, FREE)
            pool.memset(ident[:, :], 0.0).then_inc(made, 1)
            pool.memset(ident_b[:, :], 0.0).then_inc(made, 1)
            pool.memset(later_key[:, :], 0.0).then_inc(made, 1)
            pool.memset(later_key_t[:, :], 0.0).then_inc(made, 1)
            pool.memset(neg_half[:, :], -0.5).then_inc(made, 1)
            pool.wait_ge(made, 5)
            for m in (ident, ident_b):
                pool.affine_select(out=m[:, :], in_=m[:, :], compare_op=ALU.not_equal, fill=1.0, base=0,
                                   pattern=[[-1, P]], channel_multiplier=1).then_inc(made, 1)
            pool.affine_select(out=later_key[:, :], in_=later_key[:, :], compare_op=ALU.is_ge, fill=-BIG, base=0,
                               pattern=[[-1, P]], channel_multiplier=1).then_inc(made, 1)
            pool.affine_select(out=later_key_t[:, :], in_=later_key_t[:, :], compare_op=ALU.is_ge, fill=-BIG, base=0,
                               pattern=[[1, P]], channel_multiplier=-1).then_inc(made, 1)

            def inv_std(l, b, which):
                pool.wait_ge(stats_ready[l], b * 2 + which + 1)
                pool.tensor_tensor(rstd[:, :], var_eps[:, :], neg_half[:, :], ALU.pow).then_inc(rstd_ready[l], 1)

            def add_row(dst, src, row, ready, was=None):
                for t in range(T):
                    pool.tensor_tensor(dst[:, t, :], src[:, t, :], row[:, :], ALU.add).then_inc(ready, 1)

            pool.wait_ge(consts_in, N_C)
            with pool.Fori(0, B) as b:
                for l in range(2):
                    inv_std(l, b, 0)
                    if l:
                        pool.wait_ge(drained_v[0], FREE + (b + 1) * DRAINS[0]["v"])
                    else:
                        pool.wait_ge(norm_ready[0], b * 2 + 1)
                        pool.wait_ge(drained_v[1], FREE + b * DRAINS[1]["v"])
                    add_row(resb, xl1 if l else xr, bo_all[l], res_ready[l])
                    if l == 0:
                        for h in range(H):
                            if h == 0:
                                pool.wait_ge(mask_ready, FREE + b + 1)
                            pool.wait_ge(bias_in[h % G], b * 16 * NG + 16 * (h // G + 1))
                            pool.tensor_tensor(bias[:, h % G, :, :], bias[:, h % G, :, :], mask_neg[:, :, :], ALU.add)\
                                .then_inc(bias_masked, 1)
                    inv_std(l, b, 1)
                    per = 8 + 4 * l
                    add_row(resb, x1, b2_all[l], res_ready[l])
                    if l:
                        for t in range(T):
                            pool.wait_ge(res_ready[1], b * per + 5 + t)
                            pool.tensor_tensor(resb[:, t, :], resb[:, t, :], xl1[:, t, :], ALU.subtract).then_inc(res_ready[1], 1)

        @block.scalar
        def _(act):
            act.wait_ge(embed, N_EMBED)
            act.activation(emb[:, 4, :, :], emb[:, 3, :, :], ACT.Sin).then_inc(embed_act, 1)
            act.wait_ge(embed_act, 1)
            act.activation(emb[:, 5, :, :], emb[:, 4, :, :], ACT.Exp, scale=-1.0).then_inc(embed_act, 1)

            def out_of_bank(l, b, d, dst, scale, shift):
                act.wait_ge(filled[l], b * FILLS + d + 1)
                act.activation(dst, psT[:, d % 4, :], ACT.Identity, scale=scale, bias=shift).then_inc(drained_a[l], 1)

            def exps(l, b, h):
                for p in range(2):
                    j = 2 * h + p
                    act.wait_ge(t_filled[l], FREE + b * 2 * H + j + 1)
                    if h >= G:
                        act.wait_ge(pv_done[l], FREE + b * NG * T + T * (h // G - 1) + 2 * p + 2)
                    if l:
                        lo, n = (0, 896) if p == 0 else (896, 384)
                    else:
                        lo, n = p * 1024, 1024
                    src = psT[:, 2 * p:2 * p + 2, :].rearrange("p a n -> p (a n)")[:, 0:n]
                    act.activation(prob[:, h % G, lo:lo + n], src, ACT.Exp).then_inc(exped[l], 1)

            def max_out(b, g):
                act.wait_ge(m_filled, FREE + b * NG + g + 1)
                if g >= 2:
                    act.wait_ge(m_out, b * 16 * NG + 16 * (g - 1))
                act.activation(mT[:, g % 2, :], psM[0:PARTS * G * T, 0:P], ACT.Copy).then_inc(m_drained, 1)

            act.wait_ge(small_ready, N_SMALL)
            with act.Fori(0, B) as b:
                for l in range(2):
                    for c in range(C):
                        if l:
                            out_of_bank(l, b, T1 + c, hT[:, c, :], gb1[:, 0, c:c + 1], gb1[:, 1, c:c + 1])
                        else:
                            out_of_bank(l, b, T1 + c, hT[:, c, :], 1.0, 0.0)
                    for x in range(2):
                        for c in range(C):
                            out_of_bank(l, b, QK + 2 * x + c, qkf[:, x, c, :], 1.0 if x else QSCALE, bqk[l][:, x, c:c + 1])
                    if l:
                        max_out(b, 0)
                        max_out(b, 1)
                    for h in range(H):
                        exps(l, b, h)
                        if l and h % G == 0 and G <= h < 3 * G:
                            max_out(b, h // G + 1)
                    for c in range(C):
                        out_of_bank(l, b, T2 + c, hT[:, c, :], gb2[l][:, 0, c:c + 1], gb2[l][:, 1, c:c + 1])
                    for f in range(FC):
                        d = F1 + f
                        act.wait_ge(filled[l], b * FILLS + d + 1)
                        if l:
                            act.activation(gT[:, f, :], psT[:, d % 4, :], ACT.Gelu, bias=b1[1][:, f:f + 1]).then_inc(drained_a[1], 1)
                        else:
                            if f >= 2:
                                wait_drained(act, 0, b, d - 2)
                            act.activation(sig[:, f % 2, :], psT[:, d % 4, :], ACT.Sigmoid, scale=GELU_K,
                                           bias=b1k[:, f:f + 1]).then_inc(sig_ready, 1)
                act.wait_ge(y_ready, b * T + T)
                act.dma_start(out_dram[b], yout[:, :, :]).then_inc(y_out, 16)
            act.wait_ge(y_out, FREE + 16 * B)

        @block.tensor
        def _(pe):
            mparts_target = Target(pe, mparts_ready, 1, 1)
            pe.wait_ge(ada_ready, 1)
            for b in range(B):
                if b >= 2:
                    pe.wait_ge(ada_ready, b)
                for c in range(C):
                    mm = pe.matmul(psS[:, b % 2, :], act_bc[:, c, b, :], wada[:, c, :], start=c == 0, stop=c == C - 1)
                mm.then_inc(ada_filled, 1)
            pe.wait_ge(weights_in, N_W)
            pe.wait_ge(made, N_MADE)
            pe.wait_ge(small_ready, N_SMALL)

            def bank(l, b, d):
                if d >= 4:
                    wait_drained(pe, l, b, d - 4)
                elif l:
                    pe.wait_ge(drained_v[0], FREE + (b + 1) * DRAINS[0]["v"])
                else:
                    pe.wait_ge(drained_v[1], FREE + b * DRAINS[1]["v"])
                return psT[:, d % 4, :]

            def transposed(l, b, d, src, which):
                for c in range(C):
                    dst = bank(l, b, d + c)
                    for t in range(T):
                        if c == 0:
                            pe.wait_ge(norm_ready[l], b * 2 + which + 1)
                        mm = pe.transpose(dst[:, t * P:(t + 1) * P], src[:, t, c * P:(c + 1) * P], ident[:, :])
                    mm.then_inc(filled[l], 1)

            def scores(l, b, h, t):
                i = h * T + t
                if i >= 2:
                    pe.wait_ge(s_drained[l], FREE + b * H * T + i - 1)
                elif l:
                    pe.wait_ge(s_drained[0], FREE + (b + 1) * H * T)
                else:
                    pe.wait_ge(s_drained[1], FREE + b * H * T)
                n = width(t) if l else S
                mm = pe.matmul(psS[:, i % 2, 0:n], q6[0:ROWS, h, t * P:(t + 1) * P], k6[0:ROWS, h, 0:n],
                               start=True, stop=not l)
                if l:
                    mm = pe.matmul(psS[:, i % 2, t * P:n], ident_b[:, :], later_key[:, :], start=False, stop=True)
                mm.then_inc(s_filled[l], 1)

            def half_free(l, b, h, p):
                if h >= 1:
                    pe.wait_ge(exped[l], b * 2 * H + 2 * h + p - 1)

            def turn(b, h, kt):
                if kt == 0:
                    pe.wait_ge(scores_subbed, b * H * T + (h + 1) * T)
                if kt % 2 == 0:
                    half_free(0, b, h, kt // 2)
                for t in range(T):
                    mm = pe.transpose(psT[:, kt, t * P:(t + 1) * P], bias[:, h % G, t, kt * P:(kt + 1) * P], ident[:, :])
                if kt % 2:
                    mm.then_inc(t_filled[0], 1)

            def turned_scores(b, h):
                for kt in range(T):
                    n = S - kt * P
                    if kt % 2 == 0:
                        half_free(1, b, h, kt // 2)
                    dst = psT[:, 2, 256:256 + n] if kt == 3 else psT[:, kt, 0:n]
                    pe.matmul(dst, k6[0:SHIFT, h, kt * P:(kt + 1) * P], q6[0:SHIFT, h, kt * P:S], start=True, stop=False)
                    mm = pe.matmul(dst[:, 0:P], ident_b[:, :], later_key_t[:, :], start=False, stop=True)
                    if kt % 2:
                        mm.then_inc(t_filled[1], 1)

            def turn_max(b, g):
                pe.wait_ge(m_drained, FREE + b * NG + g)
                mparts_target.wait()
                pe.transpose(psM[0:PARTS * G * T, 0:P], mparts[:, g % 2, :, :].rearrange("p w r -> p (w r)"), ident_b[:, :])\
                    .then_inc(m_filled, 1)

            def values(l, b, g):
                if g:
                    pe.wait_ge(ctx_drained[l], FREE + b * NG + g)
                elif l:
                    pe.wait_ge(ctx_drained[0], FREE + (b + 1) * NG)
                else:
                    pe.wait_ge(ctx_drained[1], FREE + b * NG)
                pe.wait_ge(exped[l], b * 2 * H + 2 * G * (g + 1))
                at = [0, 512, 896, 1152]
                for kt in range(T):
                    for j in range(G):
                        lo = kt * P if l else 0
                        rhs = prob[:, j, at[kt]:at[kt] + S - lo] if l else prob[:, j, kt * S:(kt + 1) * S]
                        mm = pe.matmul(psC[j * QW:(j + 1) * QW, lo:S], vx[:, kt, g * G + j, :], rhs,
                                       start=kt == 0, stop=kt == T - 1)
                    mm.then_inc(pv_done[l], 1)

            with pe.Fori(0, B) as b:
                for l in range(2):
                    transposed(l, b, T1, xh if l else xr, 0)
                    for x, w in enumerate((wq[l], wk[l])):
                        for n in range(C):
                            d = QK + 2 * x + n
                            dst = bank(l, b, d)
                            if x == 0 and n == 0:
                                wait_drained(pe, l, b, T1 + 1)
                            for c in range(C):
                                mm = pe.matmul(dst, w[:, c, n * P:(n + 1) * P], hT[:, c, :], start=c == 0, stop=c == C - 1)
                            mm.then_inc(filled[l], 1)
                    for t in range(T):
                        dst = bank(l, b, VV + t)
                        for c in range(C):
                            mm = pe.matmul(dst[:, 0:D], hT[:, c, t * P:(t + 1) * P], wv[l][:, c, :], start=c == 0, stop=c == C - 1)
                        mm.then_inc(filled[l], 1)
                    wait_drained(pe, l, b, VV + T - 1)
                    pe.wait_ge(roles_in[l], FREE + (b + 1) * 192)
                    if l == 0:
                        for h in range(H + 1):
                            for t in range(T):
                                if h < H:
                                    if t in (0, 2, 3):
                                        scores(0, b, h, t)
                                    if t == 0:
                                        scores(0, b, h, 1)
                                if h:
                                    turn(b, h - 1, t)
                            if h and h % G == 1 and h > 1:
                                values(0, b, h // G - 1)
                        values(0, b, NG - 1)
                    else:
                        for h in range(2 * G):
                            for t in range(T):
                                scores(1, b, h, t)
                            if h == G + 1:
                                turn_max(b, 0)
                        turn_max(b, 1)
                        for h in range(H):
                            if h % G == 0:
                                pe.wait_ge(m_rows[h // G % 2], b * 32 + 16 * (h // G // 2 + 1))
                            turned_scores(b, h)
                            if h % G == 0 and G <= h < 3 * G:
                                turn_max(b, h // G + 1)
                            if h + 2 * G < H:
                                for t in range(T):
                                    scores(1, b, h + 2 * G, t)
                            if h % G == G - 1:
                                values(1, b, h // G)
                    for g in range(2):
                        pe.wait_ge(compacted[l][g], FREE + (b + 1) * 128)
                    for t in range(T):
                        dst = bank(l, b, OO + t)
                        for c in range(C):
                            mm = pe.matmul(dst[:, 0:D], ctxd[:, c, t * P:(t + 1) * P], wo[l][:, c, :], start=c == 0, stop=c == C - 1)
                        mm.then_inc(filled[l], 1)
                    transposed(l, b, T2, xh, 1)
                    for f in range(FC):
                        dst = bank(l, b, F1 + f)
                        if f == 0:
                            wait_drained(pe, l, b, T2 + 1)
                        for c in range(C):
                            mm = pe.matmul(dst, w1[l][:, c, f * P:(f + 1) * P], hT[:, c, :], start=c == 0, stop=c == C - 1)
                        mm.then_inc(filled[l], 1)
                    for t in range(T):
                        dst = bank(l, b, F2 + t)
                        for f in range(FC):
                            if t == 0:
                                wait_drained(pe, l, b, F1 + f)
                            mm = pe.matmul(dst[:, 0:D], gT[:, f, t * P:(t + 1) * P], w2[l][:, f, :], start=f == 0, stop=f == FC - 1)
                        mm.then_inc(filled[l], 1)

        @block.vector
        def _(dve):
            seconds, angle = emb[:, 0, 1, :], emb[:, 1, 0, :]
            turns, reduced, sin_cos, exp_neg, denom, silu = (emb[:, i, :, :] for i in range(2, 8))
            n = 0

            def link(ins):
                nonlocal n
                n += 1
                ins.then_inc(embed, 1)
                dve.wait_ge(embed, n)

            dve.wait_ge(ada_w_in, 64)
            link(dve.tensor_copy(emb[:, 0, 0, :], step_i[:, :]))
            link(dve.tensor_scalar(seconds, emb[:, 0, 0, :], RESCALE / NUM_STEPS, None, ALU.mult))
            link(dve.tensor_scalar(angle, seconds, freq[:, 0:1], None, ALU.mult))
            for i, offset in enumerate((0.0, 0.25)):
                link(dve.tensor_scalar(turns[:, i, :], angle, float(1 / (2 * np.pi)), offset, ALU.mult, ALU.add))
            link(dve.tensor_scalar(turns, turns, ROUND, None, ALU.add))
            link(dve.tensor_scalar(turns, turns, -ROUND, None, ALU.add))
            for k, part_of_turn in enumerate((TWO_PI_HI, TWO_PI_MID, TWO_PI_LO)):
                for i in range(2):
                    link(dve.scalar_tensor_tensor(out=reduced[:, i, :], in0=turns[:, i, :], scalar=-part_of_turn,
                                                  in1=reduced[:, i, :] if k else angle, op0=ALU.mult, op1=ALU.add))
            link(dve.tensor_scalar(reduced[:, 1, :], reduced[:, 1, :], float(np.pi / 2), None, ALU.add))
            link(dve.tensor_scalar(reduced, reduced, PI_IN, -PI_IN, ALU.min, ALU.max))
            assert n == N_EMBED
            dve.wait_ge(embed_act, 2)
            link(dve.tensor_scalar(denom, exp_neg, 1.0, None, ALU.add))
            link(dve.reciprocal(denom, denom))
            link(dve.tensor_tensor(silu, sin_cos, denom, ALU.mult))
            for c in range(C):
                for b in range(B):
                    last = dve.tensor_copy(act_bc[:, c, b, :], silu[:, c, b:b + 1].to_broadcast([P, P]))
            last.then_inc(ada_ready, 1)
            dve.wait_ge(consts_in, N_C)
            for l in range(2):
                dve.tensor_scalar(bqk[l][:, 0, :], bqk[l][:, 0, :], QSCALE, None, ALU.mult).then_inc(small_ready, 1)
            dve.tensor_scalar(b1k[:, :], b1[0][:, :], GELU_K, None, ALU.mult).then_inc(small_ready, 1)
            dve.memset(k6[ROWS:SHIFT, :, :], 1.0).then_inc(small_ready, 1)
            dve.memset(vx[:, :, :, :], 1.0).then_inc(small_ready, 1)
            for b in range(B):
                dve.wait_ge(ada_filled, b + 1)
                dve.tensor_tensor(ada[:, b, :], psS[:, b % 2, :], bada, ALU.add).then_inc(ada_ready, 1)
                dve.wait_ge(ada_ready, b + 2)
                dve.tensor_scalar(ada[:, b, 0:D], ada[:, b, 0:D], 1.0, None, ALU.add).then_inc(small_ready, 1)
            dve.wait_ge(small_ready, N_SMALL)

            measured_target = [Target(dve, measured[l], 1, 1) for l in range(2)]
            scores_target = Target(dve, s_filled[0], 1, 1)
            values_target = [Target(dve, pv_done[l], FREE + T, T) for l in range(2)]
            steps = [0, 0]

            def step(l, ins):
                steps[l] += 1
                ins.then_inc(v_step[l], 1)

            def stepped(l, b):
                dve.wait_ge(v_step[l], b * V_STEPS[l] + steps[l])

            def own_drained(l, b, d):
                dve.wait_ge(drained_v[l], FREE + b * DRAINS[l]["v"] + drains(l, d))

            def normalise(l, b, which):
                src = x1 if which else xl1 if l else xin
                for t in range(T):
                    if which:
                        own_drained(l, b, OO + t)
                    elif l:
                        own_drained(0, b, F2 + t)
                    elif t == 0:
                        dve.wait_ge(x_in, b * 16 + 16)
                    last = dve.bn_stats(stats[:, t, :], src[:, t, :])
                last.then_inc(measured[l], 1)
                measured_target[l].wait()
                for t in range(T):
                    last = dve.bn_aggr(mv[:, t, :], stats[:, t, :])
                step(l, last)
                stepped(l, b)
                dve.tensor_scalar(var_eps[:, :], mv[:, :, 1], EPS, None, ALU.add).then_inc(stats_ready[l], 1)
                dve.wait_ge(rstd_ready[l], b * 2 + which + 1)
                for t in range(T):
                    last = dve.tensor_scalar(xh[:, t, :], src[:, t, :], mv[:, t, 0:1], rstd[:, t:t + 1], ALU.subtract, ALU.mult)
                    if l == 0 and which == 0:
                        if t == T - 1:
                            last.then_inc(xin_used, 1)
                        else:
                            step(l, last)
                    elif t == T - 1:
                        last.then_inc(norm_ready[l], 1)
                if l == 0 and which == 0:
                    dve.wait_ge(xin_used, FREE + b + 1)
                    dve.wait_ge(y_out, FREE + b * 16)
                    for t in range(T):
                        step(0, dve.tensor_tensor(xr[:, t, :], xh[:, t, :], ada[:, b, 0:D], ALU.mult))
                    for t in range(T):
                        stepped(0, b)
                        last = dve.tensor_tensor(xr[:, t, :], xr[:, t, :], ada[:, b, D:2 * D], ALU.add)
                    last.then_inc(norm_ready[0], 1)

            def turn_mask(b):
                low, inf, nan = (mask_row[:, i, :] for i in range(3))
                dve.wait_ge(mask_in, b * 16 + 16)
                dve.wait_ge(bias_masked, FREE + b * H)
                step(0, dve.tensor_scalar(mask_neg[:, :, :], mask_u8[:, :, :], -BIG, None, ALU.mult))
                stepped(0, b)
                step(0, dve.tensor_reduce(low, mask_neg[:, :, :], AX_X, ALU.max))
                stepped(0, b)
                step(0, dve.tensor_scalar(inf, low, 1e30, None, ALU.mult))
                stepped(0, b)
                step(0, dve.tensor_tensor(nan, inf, inf, ALU.subtract))
                stepped(0, b)
                for t in range(T):
                    last = dve.tensor_scalar(mask_neg[:, t, :], mask_neg[:, t, :], nan[:, t:t + 1], None, ALU.add)
                last.then_inc(mask_ready, 1)

            def split(l, b, x):
                dve.wait_ge(drained_a[l], b * DRAINS[l]["a"] + drains(l, QK + 2 * x + 1))
                full, left = qkf[:, x, :, :], rem[:, x, :, :]
                high, middle, low = (part[:, x, w, :, :] for w in range(PARTS))
                step(l, dve.tensor_copy(high, full))
                stepped(l, b)
                step(l, dve.tensor_tensor(left, full, high, ALU.subtract))
                stepped(l, b)
                step(l, dve.tensor_copy(middle, left))
                stepped(l, b)
                dve.tensor_tensor(low, left, middle, ALU.subtract).then_inc(parts_ready[l], 1)

            def keep_values(l, b, t):
                dve.wait_ge(filled[l], b * FILLS + VV + t + 1)
                dve.tensor_tensor(vx[:, t, :, 0:DH], psT[:, (VV + t) % 4, 0:D].rearrange("p (h d) -> p h d", d=DH),
                                  bv_all[l][:, :].rearrange("p (h d) -> p h d", d=DH), ALU.add).then_inc(drained_v[l], 1)

            def add_bias(b, h, t):
                i = h * T + t
                if t == 0:
                    dve.wait_ge(bias_masked, FREE + b * H + h + 1)
                scores_target.wait()
                dve.tensor_tensor_reduce(bias[:, h % G, t, :], psS[:, i % 2, :], bias[:, h % G, t, :], 1.0, -3e38,
                                         ALU.add, ALU.max, rmax[:, h, t:t + 1]).then_inc(s_drained[0], 1)

            def subtract_max(b, h, t):
                i = h * T + t
                dve.wait_ge(s_drained[0], FREE + b * H * T + i + 1)
                dve.tensor_scalar(bias[:, h % G, t, :], bias[:, h % G, t, :], rmax[:, h, t:t + 1], None, ALU.subtract)\
                    .then_inc(scores_subbed, 1)

            def find_max(b, h, t):
                i = h * T + t
                dve.wait_ge(s_filled[1], b * H * T + i + 1)
                dve.tensor_reduce(rmax[:, h, t:t + 1], psS[:, i % 2, 0:width(t)], AX_X, ALU.max).then_inc(s_drained[1], 1)

            def split_max(b, g):
                m = rmax[:, g * G:(g + 1) * G, :].rearrange("p h t -> p (h t)")
                high, middle, low = (mparts[:, g % 2, w, :] for w in range(PARTS))
                left = rneg[:, g % 2, 0, :]
                dve.wait_ge(s_drained[1], FREE + b * H * T + G * T * (g + 1))
                dve.wait_ge(m_filled, FREE + b * NG + max(g - 1, 0))
                step(1, dve.tensor_scalar(high, m, -1.0, None, ALU.mult))
                stepped(1, b)
                step(1, dve.scalar_tensor_tensor(out=left, in0=m, scalar=-1.0, in1=high, op0=ALU.mult, op1=ALU.subtract))
                stepped(1, b)
                step(1, dve.tensor_copy(middle, left))
                stepped(1, b)
                dve.tensor_tensor(low, left, middle, ALU.subtract).then_inc(mparts_ready, 1)

            def divide_by_sums(l, b, g):
                if g >= 2:
                    dve.wait_ge(compacted[l][g % 2], FREE + b * 128 + 64)
                elif l:
                    dve.wait_ge(compacted[0][g % 2], FREE + (b + 1) * 128)
                else:
                    dve.wait_ge(compacted[1][g % 2], FREE + b * 128)
                values_target[l].wait()
                step(l, dve.stream_shuffle(sums[:, :], psC[:, :], [DH + i % DH for i in range(QW)]))
                stepped(l, b)
                step(l, dve.reciprocal(sums[:, :], sums[:, :]))
                stepped(l, b)
                dve.tensor_tensor(ctxn[:, g % 2, :], psC[:, :], sums[:, :], ALU.mult).then_inc(ctx_drained[l], 1)

            with dve.Fori(0, B) as b:
                for l in range(2):
                    normalise(l, b, 0)
                    if l == 0:
                        turn_mask(b)
                    for x in range(2):
                        split(l, b, x)
                    for t in range(T):
                        keep_values(l, b, t)
                    if l == 0:
                        for h in range(H):
                            for t in range(T):
                                add_bias(b, h, t)
                                if t:
                                    subtract_max(b, h, t - 1)
                            subtract_max(b, h, T - 1)
                            if h % G == 2 and h > G:
                                divide_by_sums(0, b, h // G - 1)
                    else:
                        for g in range(NG + 2):
                            if g < NG:
                                for h in range(g * G, (g + 1) * G):
                                    for t in range(T):
                                        find_max(b, h, t)
                                split_max(b, g)
                            if 2 <= g < NG + 1:
                                divide_by_sums(1, b, g - 2)
                    divide_by_sums(l, b, NG - 1)
                    dve.wait_ge(res_ready[l], b * (8 + 4 * l) + T)
                    for t in range(T):
                        dve.wait_ge(filled[l], b * FILLS + OO + t + 1)
                        dve.tensor_tensor(x1[:, t, :], psT[:, (OO + t) % 4, 0:D], resb[:, t, :], ALU.add).then_inc(drained_v[l], 1)
                    normalise(l, b, 1)
                    if l == 0:
                        for f in range(FC):
                            dve.wait_ge(sig_ready, b * FC + f + 1)
                            dve.scalar_tensor_tensor(out=gT[:, f, :], in0=psT[:, (F1 + f) % 4, :], scalar=b1[0][:, f:f + 1],
                                                     in1=sig[:, f % 2, :], op0=ALU.add, op1=ALU.mult).then_inc(drained_v[0], 1)
                    dve.wait_ge(res_ready[l], (b + 1) * (8 + 4 * l))
                    dst = yout if l else xl1
                    for t in range(T):
                        dve.wait_ge(filled[l], b * FILLS + F2 + t + 1)
                        dve.tensor_tensor(dst[:, t, :], psT[:, (F2 + t) % 4, 0:D], resb[:, t, :], ALU.add).then_inc(drained_v[l], 1)
                    if l:
                        for t in range(T):
                            own_drained(1, b, F2 + t)
                            dve.scalar_tensor_tensor(out=yout[:, t, :], in0=yout[:, t, :], scalar=gate[:, b, :], in1=xl1[:, t, :],
                                                     op0=ALU.mult, op1=ALU.add).then_inc(y_ready, 1)
            assert steps == V_STEPS, steps


_NAMES = ("x itok_B_34_63 fside_Bx16xSxS_0 condB_gatescore mask_Bx1xSxS_bk0 "
          "L0_cond_W_ada L0_cond_b_ada L0_cond_Wq L0_cond_bq L0_cond_Wk L0_cond_bk L0_cond_Wv L0_cond_bv L0_cond_Wo L0_cond_bo "
          "L0_cond_W1 L0_cond_b1 L0_cond_W2 L0_cond_b2 L0_cond_g2 L0_cond_beta2 "
          "L1_cond_Wq L1_cond_bq L1_cond_Wk L1_cond_bk L1_cond_Wv L1_cond_bv L1_cond_Wo L1_cond_bo "
          "L1_cond_W1 L1_cond_b1 L1_cond_W2 L1_cond_b2 L1_cond_gamma1 L1_cond_beta1 L1_cond_gamma2 L1_cond_beta2").split()


def kernel(**inputs):
    import numpy as _np
    import concourse.bacc as _bacc
    from concourse import mybir as _mybir
    from concourse.bass_utils import run_bass_kernel_spmd as _run

    nc = _bacc.Bacc("TRN2", target_bir_lowering=False, num_devices=1)
    arrays, args = {}, {}
    for name in _NAMES:
        v = _np.ascontiguousarray(inputs[name])
        arrays[f"in_{name}"] = v
        args[name] = nc.dram_tensor(f"in_{name}", v.shape, _mybir.dt.from_np(v.dtype), kind="ExternalInput").ap()
    out = nc.dram_tensor("out", (B, S, D), F32, kind="ExternalOutput").ap()
    two_layers(nc, args, out)
    r = _run(nc, [arrays], core_ids=[0])
    return r.results[0]["out"]
```

```python
from contextlib import ExitStack

import numpy as np

import concourse.bass as bass
from concourse import mybir

F32 = mybir.dt.float32
BF16 = mybir.dt.bfloat16
U8 = mybir.dt.uint8
I32 = mybir.dt.int32
ALU = mybir.AluOpType
ACT = mybir.ActivationFunctionType
AX_X = mybir.AxisListType.X

P = 128
B, S, D = 4, 512, 256
H, DH, F = 16, 16, 1024
T = S // P
C = D // P
FC = F // P
G = 4
NG = H // G
QW = 32
PARTS = 3
Q_ROLE = [0, 0, 1, 0, 2, 1]
K_ROLE = [0, 1, 0, 2, 0, 1]
ROWS = DH * len(Q_ROLE)
SHIFT = ROWS + PARTS
QSCALE = DH ** -0.5
EPS = 1e-5
BIG = 1e37
GELU_K = 1.702
NUM_STEPS, RESCALE = 100.0, 4000.0
ROUND = 12582912.0
TWO_PI_HI, TWO_PI_MID = 6.28125, 0.0019350051879882812
TWO_PI_LO = float(2 * np.pi - TWO_PI_HI - TWO_PI_MID)
PI_IN = 3.1415925

ROLES_IN = 16 * 2 * len(Q_ROLE)
FREE = 1

T1, QK, VV, OO, T2, F1, F2 = 0, 2, 6, 10, 14, 16, 24
FILLS = 28


def width(t):
    return (t + 1) * P


A_TILES = (1, 3)
V_TILES = tuple(t for t in range(T) if t not in A_TILES)


def drainer(layer, d):
    if d < VV or T2 <= d < F1:
        return "a"
    if F1 <= d < F2:
        return "a" if layer else "v"
    return "v"


def drains(layer, d):
    return sum(drainer(layer, e) == drainer(layer, d) for e in range(d + 1))


DRAINS = [{e: sum(drainer(l, d) == e for d in range(FILLS)) for e in "av"} for l in range(2)]
M_USES = [[("raw", 0), ("raw", 1), ("channels", 0), ("raw", 2), ("raw", 3), ("channels", 1)],
          [("max", 0), ("max", 1), ("max", 2), ("raw", 0), ("max", 3), ("raw", 1), ("channels", 0), ("raw", 2),
           ("raw", 3), ("channels", 1)]]
V_STEPS = [25, 30]


def two_layers(nc, a, out):
    freqs = np.exp(np.arange(P, dtype=np.float32) * np.float32(-np.log(10000.0) / (P - 1)))
    freq_table = nc.inline_tensor(freqs.astype(np.float32).reshape(P, 1))
    freq_dram = freq_table.ap()
    part_dram = nc.dram_tensor("part_dram", (2, PARTS, D, S), BF16, kind="Internal").ap()
    max_dram = nc.dram_tensor("max_dram", (NG, PARTS * G * T, P), BF16, kind="Internal").ap()
    bias_dram = a["fside_Bx16xSxS_0"].rearrange("b h (t p) k -> (b h) p t k", p=P)
    x_dram = a["x"].rearrange("b (t p) d -> b p t d", p=P)
    out_dram = out.rearrange("b (t p) d -> b p t d", p=P)
    mask_dram = a["mask_Bx1xSxS_bk0"].rearrange("b o (t p) k -> (b o) p t k", p=P)
    par = [{k.removeprefix(f"L{l}_cond_"): v for k, v in a.items() if k.startswith(f"L{l}_")} for l in range(2)]
    gam = [par[0]["g2"], par[1]["gamma2"]]
    bet = [par[0]["beta2"], par[1]["beta2"]]

    nc.disable_value_cache = True

    with ExitStack() as ctx:
        def sb(name, shape, dt=F32):
            return ctx.enter_context(nc.sbuf_tensor(name, shape, dt))

        def ps(name, shape, dt=F32):
            return ctx.enter_context(nc.psum_tensor(name, shape, dt))

        def sem(name):
            return ctx.enter_context(nc.semaphore(name))

        def sem2(name):
            return [sem(f"{name}{l}") for l in range(2)]

        wq, wk, wv, wo = ([sb(f"{n}{l}", [P, C, D]) for l in range(2)] for n in ("wq", "wk", "wv", "wo"))
        w1 = [sb(f"w1_{l}", [P, C, F]) for l in range(2)]
        w2 = [sb(f"w2_{l}", [P, FC, D]) for l in range(2)]
        bqk = [sb(f"bqk{l}", [P, 2, C]) for l in range(2)]
        b1 = [sb(f"b1_{l}", [P, FC]) for l in range(2)]
        b1k = sb("b1k", [P, FC])
        gb1 = sb("gb1", [P, 2, C])
        gb2 = [sb(f"gb2_{l}", [P, 2, C]) for l in range(2)]
        bv_all = [sb(f"bv_all{l}", [P, D]) for l in range(2)]
        bo_all = [sb(f"bo_all{l}", [P, D]) for l in range(2)]
        b2_all = [sb(f"b2_all{l}", [P, D]) for l in range(2)]
        gate = sb("gate", [P, B, 1])
        ada = sb("ada", [P, B, 2 * D])
        ident = sb("ident", [P, P])
        ident_b = sb("ident_b", [P, P], BF16)
        later_key = sb("later_key", [P, P], BF16)
        later_key_t = sb("later_key_t", [P, P], BF16)
        free = sb("free", [P, 32])
        freq = sb("freq", [P, 1])
        step_i = sb("step_i", [P, B], I32)
        emb = sb("emb", [P, 8, 2, B])
        mask_u8 = sb("mask_u8", [P, T, S], U8)
        mask_neg = sb("mask_neg", [P, T, S])
        mask_row = sb("mask_row", [P, 3, T])
        xin, xh, xr, resb, x1, xl1 = (sb(n, [P, T, D]) for n in ("xin", "xh", "xr", "resb", "x1", "xl1"))
        yout = xr
        stats = sb("stats", [P, T, 6])
        mv = sb("mv", [P, T, 2])
        var_eps, rstd, neg_half = (sb(n, [P, T]) for n in ("var_eps", "rstd", "neg_half"))
        hT = sb("hT", [P, C, S])
        q6 = sb("q6", [P, H, S], BF16)
        k6 = sb("k6", [P, H, S], BF16)
        vx = sb("vx", [P, T, H, QW])
        bias = sb("bias", [P, G, T, S])
        rmax = sb("rmax", [P, H, T])
        rneg = sb("rneg", [P, 2, 2, G * T])
        mparts = sb("mparts", [P, 2, PARTS, G * T], BF16)
        mT = sb("mT", [PARTS * G * T, 2, P], BF16)
        craw = hT
        ctxn = x1
        ctxd = xh[:, :, :].rearrange("p (c a) n -> p c (a n)", c=C)
        inv_sum = sb("inv_sum", [P, T, G])
        work = sb("work", [P, G * T * S])
        prob = work[:, :].rearrange("p (g n) -> p g n", g=G)
        qkf = work[:, 0:2048].rearrange("p (x c n) -> p x c n", x=2, c=C)
        rem = work[:, 2048:4096].rearrange("p (x c n) -> p x c n", x=2, c=C)
        part = work[:, 4096:7168].bitcast(BF16).rearrange("p (x w c n) -> p x w c n", x=2, w=PARTS, c=C)
        gT = work[:, 0:4096].rearrange("p (f n) -> p f n", f=FC)
        sig = work[:, 4096:5120].rearrange("p (i n) -> p i n", i=2)
        wada = work[:, 0:1024].rearrange("p (c n) -> p c n", c=C)
        bada = work[:, 1024:1536]
        act_bc = work[:, 2048:3072].rearrange("p (c b n) -> p c b n", c=C, b=B)

        psS = ps("psS", [P, 2, S])
        psT = ps("psT", [P, 4, S])
        psC = ps("psC", [P, S])
        psM = ps("psM", [P, S])
        s_banks = [[psS[:, 0, :], psS[:, 1, :]], [psS[:, 0, :], psS[:, 1, :], psT[:, 3, :]]]

        weights_in, ada_w_in, consts_in = sem("weights_in"), sem("ada_w_in"), sem("consts_in")
        made = sem("made")
        embed, embed_act, ada_filled, ada_ready = (sem(n) for n in ("embed", "embed_act", "ada_filled", "ada_ready"))
        small_ready = sem("small_ready")
        x_in, mask_in, mask_ready, xin_used = sem("x_in"), sem("mask_in"), sem("mask_ready"), sem("xin_used")
        bias_in = [sem(f"bias_in{s}") for s in range(G)]
        bias_masked, subbed_v, subbed_a = sem("bias_masked"), sem("subbed_v"), sem("subbed_a")
        v_step, measured = sem2("v_step"), sem2("measured")
        stats_ready, rstd_ready, norm_ready = sem2("stats_ready"), sem2("rstd_ready"), sem2("norm_ready")
        res_ready = sem2("res_ready")
        filled, drained_a, drained_v = sem2("filled"), sem2("drained_a"), sem2("drained_v")
        parts_ready, parts_out = sem2("parts_ready"), sem2("parts_out")
        roles_in = [[sem(f"roles_in{l}_{c}") for c in range(C)] for l in range(2)]
        s_filled, s_drained = sem2("s_filled"), sem2("s_drained")
        t_filled, exped = sem2("t_filled"), sem2("exped")
        pv_done = sem2("pv_done")
        raw_ready, raw_turned, ctx_normed = sem2("raw_ready"), sem2("raw_turned"), sem2("ctx_normed")
        ctx_turned, ctx_ready = sem2("ctx_turned"), sem2("ctx_ready")
        mparts_ready, m_filled, m_drained = sem("mparts_ready"), sem("m_filled"), sem("m_drained")
        m_out = sem("m_out")
        m_rows = [sem(f"m_rows{g}") for g in range(2)]
        sig_ready = sem("sig_ready")
        y_ready, y_out = sem("y_ready"), sem("y_out")

        N_W, N_C, N_MADE, N_EMBED, N_SMALL = 16 * 12, 16 * 19, 9, 15, 5 + B

        def wait_drained(eng, l, b, d):
            e = drainer(l, d)
            if e == "a":
                eng.wait_ge(drained_a[l], b * DRAINS[l][e] + drains(l, d))
            else:
                eng.wait_ge(drained_v[l], FREE + b * DRAINS[l][e] + drains(l, d))

        class Target:

            def __init__(self, eng, sem, first, step):
                self.eng, self.sem, self.step = eng, sem, step
                self.reg = eng.alloc_register()
                eng.reg_mov(self.reg, first)

            def wait(self):
                self.eng.wait_ge(self.sem, self.reg)
                self.eng.reg_add(self.reg, self.reg, self.step)

        block = ctx.enter_context(nc.Block())

        @block.sync
        def _(sp):
            def col(v, n):
                return v.rearrange("(c p) -> p c", p=P)[:, 0:n]

            def row_all(v, n):
                return v.rearrange("(a n) -> a n", a=1).to_broadcast([P, n])

            def load_first():
                sp.dma_start(xin[:, :, :], x_dram[0]).then_inc(x_in, 16)
                sp.dma_start(mask_u8[:, :, :], mask_dram[0]).then_inc(mask_in, 16)

            load_first()
            sp.dma_start(wada, par[0]["W_ada"].rearrange("(c p) n -> p c n", p=P)).then_inc(ada_w_in, 16)
            sp.dma_start(bada, row_all(par[0]["b_ada"], 2 * D)).then_inc(ada_w_in, 16)
            sp.dma_start(step_i[:, :], a["itok_B_34_63"].rearrange("(a n) -> a n", a=1).to_broadcast([P, B])).then_inc(ada_w_in, 16)
            sp.dma_start(freq[:, :], freq_dram).then_inc(ada_w_in, 16)
            sp.dma_start(gate[:, :, 0], row_all(a["condB_gatescore"], B)).then_inc(consts_in, 16)
            n = 16
            for l in range(2):
                loads = [(bqk[l][:, 0, :], col(par[l]["bq"], C)), (bqk[l][:, 1, :], col(par[l]["bk"], C)),
                         (b1[l][:, :], col(par[l]["b1"], FC)), (gb2[l][:, 0, :], col(gam[l], C)),
                         (gb2[l][:, 1, :], col(bet[l], C)), (bv_all[l][:, :], row_all(par[l]["bv"], D)),
                         (bo_all[l][:, :], row_all(par[l]["bo"], D)), (b2_all[l][:, :], row_all(par[l]["b2"], D))]
                if l:
                    loads += [(gb1[:, 0, :], col(par[1]["gamma1"], C)), (gb1[:, 1, :], col(par[1]["beta1"], C))]
                for dst, src in loads:
                    with nc.allow_non_contiguous_dma(reason="per-channel columns, once"):
                        sp.dma_start(dst, src).then_inc(consts_in, 16)
                    n += 16
            assert n == N_C
            for h in range(2):
                sp.dma_start(bias[:, h, :, :], bias_dram[h]).then_inc(bias_in[h], 16)
            n = 0
            for l in range(2):
                for dst, name in ((wq, "Wq"), (wk, "Wk"), (wv, "Wv"), (wo, "Wo"), (w1, "W1"), (w2, "W2")):
                    sp.dma_start(dst[l][:, :, :], par[l][name].rearrange("(c p) n -> p c n", p=P)).then_inc(weights_in, 16)
                    n += 16
            assert n == N_W
            for h in range(2, G):
                sp.dma_start(bias[:, h, :, :], bias_dram[h]).then_inc(bias_in[h], 16)

            def to_roles(l, b):
                for c in range(C):
                    if l:
                        sp.wait_ge(roles_in[0][c], FREE + (b + 1) * ROLES_IN)
                        sp.wait_ge(pv_done[0], FREE + (b + 1) * NG * T)
                    else:
                        sp.wait_ge(roles_in[1][c], FREE + b * ROLES_IN)
                        sp.wait_ge(pv_done[1], FREE + b * NG * T)
                    sp.wait_ge(parts_ready[l], b * C + c + 1)
                    for x in range(2):
                        sp.dma_start(part_dram[x].rearrange("w (c p) n -> c p w n", p=P)[c], part[:, x, :, c, :]).then_inc(parts_out[l], 16)
                    sp.wait_ge(parts_out[l], b * 32 * C + 32 * (c + 1))
                    for x, (dst, roles) in enumerate(((q6, Q_ROLE), (k6, K_ROLE))):
                        for r, w in enumerate(roles):
                            sp.dma_start(dst[r * DH:(r + 1) * DH, c * H // C:(c + 1) * H // C, :],
                                         part_dram[x, w, c * P:(c + 1) * P].rearrange("(h d) n -> d h n", d=DH)).then_inc(roles_in[l][c], 16)

            def max_rows(b, g):
                sp.wait_ge(m_drained, FREE + b * NG + g + 1)
                sp.dma_start(max_dram[g], mT[:, g % 2, :]).then_inc(m_out, 16)
                sp.wait_ge(m_out, b * 16 * NG + 16 * (g + 1))
                sp.dma_start(q6[ROWS:SHIFT, g * G:(g + 1) * G, :].rearrange("p h (t k) -> p (h t) k", k=P),
                             max_dram[g].rearrange("(w r) k -> w r k", w=PARTS)).then_inc(m_rows[g % 2], 16)

            def load_bias(b, h):
                sp.dma_start(bias[:, h % G, :, :], bias_dram[b * H + h]).then_inc(bias_in[h % G], 16)

            def load_rows(b):
                sp.dma_start(xin[:, :, :], x_dram[b]).then_inc(x_in, 16)
                sp.dma_start(mask_u8[:, :, :], mask_dram[b]).then_inc(mask_in, 16)

            def batch(b, more):
                to_roles(0, b)
                for h in range(G, H):
                    sp.wait_ge(t_filled[0], FREE + b * 2 * H + 2 * (h - G) + 2)
                    load_bias(b, h)
                to_roles(1, b)
                for g in range(NG):
                    max_rows(b, g)
                    if more and g in (1, 2):
                        for h in range(2 * (g - 1), 2 * g):
                            sp.wait_ge(t_filled[0], FREE + b * 2 * H + 2 * (H - G + h) + 2)
                            load_bias(b + 1, h)
                if more:
                    sp.wait_ge(mask_ready, FREE + b + 1)
                    load_rows(b + 1)

            with sp.Fori(0, B - 1) as b:
                batch(b, True)
            batch(B - 1, False)

        @block.gpsimd
        def _(pool):
            from_free = [xin_used, mask_ready, m_drained, m_filled, y_out, bias_masked, *t_filled, *roles_in[0], *roles_in[1], *pv_done,
                         *drained_v, *s_drained, *raw_ready, *ctx_normed, *ctx_ready]
            for i, s in enumerate(from_free):
                pool.memset(free[:, i:i + 1], 0.0).then_inc(s, FREE)
            pool.memset(ident[:, :], 0.0).then_inc(made, 1)
            pool.memset(ident_b[:, :], 0.0).then_inc(made, 1)
            pool.memset(later_key[:, :], 0.0).then_inc(made, 1)
            pool.memset(later_key_t[:, :], 0.0).then_inc(made, 1)
            pool.memset(neg_half[:, :], -0.5).then_inc(made, 1)
            pool.wait_ge(made, 5)
            for m in (ident, ident_b):
                pool.affine_select(out=m[:, :], in_=m[:, :], compare_op=ALU.not_equal, fill=1.0, base=0,
                                   pattern=[[-1, P]], channel_multiplier=1).then_inc(made, 1)
            pool.affine_select(out=later_key[:, :], in_=later_key[:, :], compare_op=ALU.is_ge, fill=-BIG, base=0,
                               pattern=[[-1, P]], channel_multiplier=1).then_inc(made, 1)
            pool.affine_select(out=later_key_t[:, :], in_=later_key_t[:, :], compare_op=ALU.is_ge, fill=-BIG, base=0,
                               pattern=[[1, P]], channel_multiplier=-1).then_inc(made, 1)

            def inv_std(l, b, which):
                for t in range(T):
                    pool.wait_ge(stats_ready[l], b * 2 * T + which * T + t + 1)
                    pool.tensor_tensor(rstd[:, t:t + 1], var_eps[:, t:t + 1], neg_half[:, t:t + 1], ALU.pow).then_inc(rstd_ready[l], 1)

            def add_row(dst, src, row, ready, was=None):
                for t in range(T):
                    pool.tensor_tensor(dst[:, t, :], src[:, t, :], row[:, :], ALU.add).then_inc(ready, 1)

            pool.wait_ge(consts_in, N_C)
            with pool.Fori(0, B) as b:
                for l in range(2):
                    inv_std(l, b, 0)
                    if l:
                        pool.wait_ge(drained_v[0], FREE + (b + 1) * DRAINS[0]["v"])
                    else:
                        pool.wait_ge(norm_ready[0], b * 2 * T + T)
                        pool.wait_ge(drained_v[1], FREE + b * DRAINS[1]["v"])
                    add_row(resb, xl1 if l else xr, bo_all[l], res_ready[l])
                    if l == 0:
                        for h in range(H):
                            if h == 0:
                                pool.wait_ge(mask_ready, FREE + b + 1)
                            pool.wait_ge(bias_in[h % G], b * 16 * NG + 16 * (h // G + 1))
                            pool.tensor_tensor(bias[:, h % G, :, :], bias[:, h % G, :, :], mask_neg[:, :, :], ALU.add)\
                                .then_inc(bias_masked, 1)
                    inv_std(l, b, 1)
                    per = 8 + 4 * l
                    add_row(resb, x1, b2_all[l], res_ready[l])
                    if l:
                        for t in range(T):
                            pool.wait_ge(res_ready[1], b * per + 5 + t)
                            pool.tensor_tensor(resb[:, t, :], resb[:, t, :], xl1[:, t, :], ALU.subtract).then_inc(res_ready[1], 1)

        @block.scalar
        def _(act):
            act.wait_ge(embed, N_EMBED)
            act.activation(emb[:, 4, :, :], emb[:, 3, :, :], ACT.Sin).then_inc(embed_act, 1)
            act.wait_ge(embed_act, 1)
            act.activation(emb[:, 5, :, :], emb[:, 4, :, :], ACT.Exp, scale=-1.0).then_inc(embed_act, 1)

            def out_of_bank(l, b, d, dst, scale, shift):
                act.wait_ge(filled[l], b * FILLS + d + 1)
                act.activation(dst, psT[:, d % 4, :], ACT.Identity, scale=scale, bias=shift).then_inc(drained_a[l], 1)

            def from_max(b, h, t):
                act.wait_ge(s_drained[0], FREE + b * H * T + h * T + t + 1)
                act.activation(bias[:, h % G, t, :], bias[:, h % G, t, :], ACT.Identity, scale=-1.0,
                               bias=rmax[:, h, t:t + 1]).then_inc(subbed_a, 1)

            def keep_context(l, b, g):
                act.wait_ge(pv_done[l], FREE + b * NG * T + T * (g + 1))
                if g >= 2:
                    act.wait_ge(raw_turned[l], b * NG + g - 1)
                act.activation(craw[:, g % 2, :], psC[:, :], ACT.Copy).then_inc(raw_ready[l], 1)

            def keep_channels(l, b, c):
                act.wait_ge(ctx_turned[l], b * C + c + 1)
                act.activation(ctxd[:, c, :], psM[:, :], ACT.Copy).then_inc(ctx_ready[l], 1)

            def exps(l, b, h, halves=(0, 1)):
                for p in halves:
                    j = 2 * h + p
                    act.wait_ge(t_filled[l], FREE + b * 2 * H + j + 1)
                    if h >= G:
                        act.wait_ge(pv_done[l], FREE + b * NG * T + T * (h // G - 1) + 2 * p + 2)
                    if l:
                        lo, n = (0, 896) if p == 0 else (896, 384)
                    else:
                        lo, n = p * 1024, 1024
                    src = psT[:, 2 * p:2 * p + 2, :].rearrange("p a n -> p (a n)")[:, 0:n]
                    act.activation(prob[:, h % G, lo:lo + n], src, ACT.Exp, scale=1.0 if l else -1.0).then_inc(exped[l], 1)

            def max_out(b, g):
                act.wait_ge(m_filled, FREE + b * NG + g + 1)
                if g >= 2:
                    act.wait_ge(m_out, b * 16 * NG + 16 * (g - 1))
                act.activation(mT[:, g % 2, :], psM[:, :].bitcast(BF16)[0:PARTS * G * T, 0:P], ACT.Copy).then_inc(m_drained, 1)

            act.wait_ge(small_ready, N_SMALL)
            with act.Fori(0, B) as b:
                for l in range(2):
                    for c in range(C):
                        if l:
                            out_of_bank(l, b, T1 + c, hT[:, c, :], gb1[:, 0, c:c + 1], gb1[:, 1, c:c + 1])
                        else:
                            out_of_bank(l, b, T1 + c, hT[:, c, :], 1.0, 0.0)
                    for c in range(C):
                        for x in range(2):
                            out_of_bank(l, b, QK + 2 * c + x, qkf[:, x, c, :], 1.0 if x else QSCALE, bqk[l][:, x, c:c + 1])
                    if l:
                        max_out(b, 0)
                        max_out(b, 1)
                    act.wait_ge(parts_out[l], (b + 1) * 32 * C)
                    if l == 0:
                        for h in range(H + 1):
                            if h < H:
                                from_max(b, h, A_TILES[0])
                            if h:
                                exps(0, b, h - 1, (0,))
                            if h < H:
                                from_max(b, h, A_TILES[1])
                            if h:
                                exps(0, b, h - 1, (1,))
                            if h % G == 1 and h > 1:
                                keep_context(0, b, h // G - 1)
                            if h == 3 * G:
                                keep_channels(0, b, 0)
                        keep_context(0, b, NG - 1)
                    else:
                        for h in range(H):
                            exps(1, b, h)
                            if h % G == 0 and G <= h < 3 * G:
                                max_out(b, h // G + 1)
                            if h % G == 1 and h > 1:
                                keep_context(1, b, h // G - 1)
                            if h == 3 * G - 1:
                                keep_channels(1, b, 0)
                        keep_context(1, b, NG - 1)
                    keep_channels(l, b, 1)
                    for c in range(C):
                        out_of_bank(l, b, T2 + c, hT[:, c, :], gb2[l][:, 0, c:c + 1], gb2[l][:, 1, c:c + 1])
                    for f in range(FC):
                        d = F1 + f
                        act.wait_ge(filled[l], b * FILLS + d + 1)
                        if l:
                            act.activation(gT[:, f, :], psT[:, d % 4, :], ACT.Gelu, bias=b1[1][:, f:f + 1]).then_inc(drained_a[1], 1)
                        else:
                            if f >= 2:
                                wait_drained(act, 0, b, d - 2)
                            act.activation(sig[:, f % 2, :], psT[:, d % 4, :], ACT.Sigmoid, scale=GELU_K,
                                           bias=b1k[:, f:f + 1]).then_inc(sig_ready, 1)
                act.wait_ge(y_ready, b * T + T)
                act.dma_start(out_dram[b], yout[:, :, :]).then_inc(y_out, 16)
            act.wait_ge(y_out, FREE + 16 * B)

        @block.tensor
        def _(pe):
            mparts_target = Target(pe, mparts_ready, 1, 1)
            pe.wait_ge(ada_ready, 1)
            for b in range(B):
                if b >= 2:
                    pe.wait_ge(ada_ready, b)
                for c in range(C):
                    mm = pe.matmul(psS[:, b % 2, :], act_bc[:, c, b, :], wada[:, c, :], start=c == 0, stop=c == C - 1)
                mm.then_inc(ada_filled, 1)
            pe.wait_ge(weights_in, N_W)
            pe.wait_ge(made, N_MADE)
            pe.wait_ge(small_ready, N_SMALL)

            def bank(l, b, d):
                if d >= 4:
                    wait_drained(pe, l, b, d - 4)
                elif l:
                    pe.wait_ge(drained_v[0], FREE + (b + 1) * DRAINS[0]["v"])
                else:
                    pe.wait_ge(drained_v[1], FREE + b * DRAINS[1]["v"])
                return psT[:, d % 4, :]

            def transposed(l, b, d, src, which):
                dst = [bank(l, b, d + c) for c in range(C)]
                for t in range(T):
                    pe.wait_ge(norm_ready[l], b * 2 * T + which * T + t + 1)
                    for c in range(C):
                        mm = pe.transpose(dst[c][:, t * P:(t + 1) * P], src[:, t, c * P:(c + 1) * P], ident[:, :])
                        if t == T - 1:
                            mm.then_inc(filled[l], 1)

            def scores(l, b, h, t):
                i = h * T + t
                banks = s_banks[l]
                if i >= len(banks):
                    pe.wait_ge(s_drained[l], FREE + b * H * T + i - len(banks) + 1)
                elif l:
                    pe.wait_ge(s_drained[0], FREE + (b + 1) * H * T)
                else:
                    pe.wait_ge(s_drained[1], FREE + b * H * T)
                n = width(t) if l else S
                dst = banks[i % len(banks)]
                mm = pe.matmul(dst[:, 0:n], q6[0:ROWS, h, t * P:(t + 1) * P], k6[0:ROWS, h, 0:n], start=True, stop=not l)
                if l:
                    mm = pe.matmul(dst[:, t * P:n], ident_b[:, :], later_key[:, :], start=False, stop=True)
                mm.then_inc(s_filled[l], 1)

            def half_free(l, b, h, p):
                if h >= 1:
                    pe.wait_ge(exped[l], b * 2 * H + 2 * h + p - 1)

            def turn(b, h, kt):
                if kt == 0:
                    pe.wait_ge(subbed_v, b * H * len(V_TILES) + (h + 1) * len(V_TILES))
                    pe.wait_ge(subbed_a, b * H * len(A_TILES) + (h + 1) * len(A_TILES))
                if kt % 2 == 0:
                    half_free(0, b, h, kt // 2)
                for t in range(T):
                    mm = pe.transpose(psT[:, kt, t * P:(t + 1) * P], bias[:, h % G, t, kt * P:(kt + 1) * P], ident[:, :])
                if kt % 2:
                    mm.then_inc(t_filled[0], 1)

            def turned_scores(b, h, tiles):
                for kt in tiles:
                    n = S - kt * P
                    if kt % 2 == 0:
                        half_free(1, b, h, kt // 2)
                    dst = psT[:, 2, 256:256 + n] if kt == 3 else psT[:, kt, 0:n]
                    pe.matmul(dst, k6[0:SHIFT, h, kt * P:(kt + 1) * P], q6[0:SHIFT, h, kt * P:S], start=True, stop=False)
                    mm = pe.matmul(dst[:, 0:P], ident_b[:, :], later_key_t[:, :], start=False, stop=True)
                    if kt % 2:
                        mm.then_inc(t_filled[1], 1)

            def bank_m_free(l, b, use):
                kind, n = M_USES[l][use - 1] if use else M_USES[1 - l][-1]
                if use == 0:
                    l, b = 1 - l, (b if l else b - 1)
                if kind == "max":
                    pe.wait_ge(m_drained, FREE + b * NG + n + 1)
                elif kind == "raw":
                    pe.wait_ge(ctx_normed[l], FREE + b * NG + n + 1)
                else:
                    pe.wait_ge(ctx_ready[l], FREE + b * C + n + 1)

            def turn_context(l, b, g):
                bank_m_free(l, b, M_USES[l].index(("raw", g)))
                pe.wait_ge(raw_ready[l], FREE + b * NG + g + 1)
                for t in range(T):
                    mm = pe.transpose(psM[:, t * P:(t + 1) * P], craw[:, g % 2, t * P:(t + 1) * P], ident[:, :])
                mm.then_inc(raw_turned[l], 1)

            def turn_channels(l, b, c):
                bank_m_free(l, b, M_USES[l].index(("channels", c)))
                pe.wait_ge(ctx_normed[l], FREE + b * NG + 2 * c + 2)
                for t in range(T):
                    mm = pe.transpose(psM[:, t * P:(t + 1) * P], ctxn[:, t, c * P:(c + 1) * P], ident[:, :])
                mm.then_inc(ctx_turned[l], 1)

            def turn_max(b, g):
                bank_m_free(1, b, M_USES[1].index(("max", g)))
                mparts_target.wait()
                pe.transpose(psM[:, :].bitcast(BF16)[0:PARTS * G * T, 0:P], mparts[:, g % 2, :, :].rearrange("p w r -> p (w r)"), ident_b[:, :])\
                    .then_inc(m_filled, 1)

            def values(l, b, g):
                if g:
                    pe.wait_ge(raw_ready[l], FREE + b * NG + g)
                elif l:
                    pe.wait_ge(raw_ready[0], FREE + (b + 1) * NG)
                else:
                    pe.wait_ge(raw_ready[1], FREE + b * NG)
                pe.wait_ge(exped[l], b * 2 * H + 2 * G * (g + 1))
                at = [0, 512, 896, 1152]
                for kt in range(T):
                    for j in range(G):
                        lo = kt * P if l else 0
                        rhs = prob[:, j, at[kt]:at[kt] + S - lo] if l else prob[:, j, kt * S:(kt + 1) * S]
                        mm = pe.matmul(psC[j * QW:(j + 1) * QW, lo:S], vx[:, kt, g * G + j, :], rhs,
                                       start=kt == 0, stop=kt == T - 1)
                    mm.then_inc(pv_done[l], 1)

            with pe.Fori(0, B) as b:
                for l in range(2):
                    transposed(l, b, T1, xh if l else xr, 0)
                    for n in range(C):
                        for x, w in enumerate((wq[l], wk[l])):
                            dst = bank(l, b, QK + 2 * n + x)
                            if x == 0 and n == 0:
                                wait_drained(pe, l, b, T1 + 1)
                            for c in range(C):
                                mm = pe.matmul(dst, w[:, c, n * P:(n + 1) * P], hT[:, c, :], start=c == 0, stop=c == C - 1)
                            mm.then_inc(filled[l], 1)
                    for t in range(T):
                        dst = bank(l, b, VV + t)
                        for c in range(C):
                            mm = pe.matmul(dst[:, 0:D], hT[:, c, t * P:(t + 1) * P], wv[l][:, c, :], start=c == 0, stop=c == C - 1)
                        mm.then_inc(filled[l], 1)
                    wait_drained(pe, l, b, VV + T - 1)
                    if l == 0:
                        for h in range(H + 1):
                            if h < H and h % (H // C) == 0:
                                pe.wait_ge(roles_in[0][h * C // H], FREE + (b + 1) * ROLES_IN)
                            for t in range(T):
                                if h < H:
                                    if t in (0, 2, 3):
                                        scores(0, b, h, t)
                                    if t == 0:
                                        scores(0, b, h, 1)
                                if h:
                                    turn(b, h - 1, t)
                            if h % G == 1 and h > 1:
                                values(0, b, h // G - 1)
                            if h % G == 2 and h > 2:
                                turn_context(0, b, h // G - 1)
                            if h == 3 * G - 1:
                                turn_channels(0, b, 0)
                        values(0, b, NG - 1)
                    else:
                        for h in range(2 * G):
                            if h % (H // C) == 0:
                                pe.wait_ge(roles_in[1][h * C // H], FREE + (b + 1) * ROLES_IN)
                            for t in range(T):
                                scores(1, b, h, t)
                            if h == G + 1:
                                turn_max(b, 0)
                        turn_max(b, 1)
                        pe.wait_ge(roles_in[1][1], FREE + (b + 1) * ROLES_IN)
                        for h in range(H):
                            if h % G == 0:
                                pe.wait_ge(m_rows[h // G % 2], b * 32 + 16 * (h // G // 2 + 1))
                            for t, tiles in enumerate(((0,), (1,), (2, 3), ())):
                                turned_scores(b, h, tiles)
                                if h + 2 * G < H:
                                    scores(1, b, h + 2 * G, t)
                            if h % G == 0 and G <= h < 3 * G:
                                turn_max(b, h // G + 1)
                            if h % G == 0 and h:
                                values(1, b, h // G - 1)
                            if h % G == 1 and h > 1:
                                turn_context(1, b, h // G - 1)
                            if h == 3 * G - 2:
                                turn_channels(1, b, 0)
                        values(1, b, NG - 1)
                    turn_context(l, b, NG - 1)
                    turn_channels(l, b, 1)
                    for t in range(T):
                        dst = bank(l, b, OO + t)
                        if t == 0:
                            pe.wait_ge(ctx_ready[l], FREE + (b + 1) * C)
                        for c in range(C):
                            mm = pe.matmul(dst[:, 0:D], ctxd[:, c, t * P:(t + 1) * P], wo[l][:, c, :], start=c == 0, stop=c == C - 1)
                        mm.then_inc(filled[l], 1)
                    transposed(l, b, T2, xh, 1)
                    for f in range(FC):
                        dst = bank(l, b, F1 + f)
                        if f == 0:
                            wait_drained(pe, l, b, T2 + 1)
                        for c in range(C):
                            mm = pe.matmul(dst, w1[l][:, c, f * P:(f + 1) * P], hT[:, c, :], start=c == 0, stop=c == C - 1)
                        mm.then_inc(filled[l], 1)
                    for t in range(T):
                        dst = bank(l, b, F2 + t)
                        for f in range(FC):
                            if t == 0:
                                wait_drained(pe, l, b, F1 + f)
                            mm = pe.matmul(dst[:, 0:D], gT[:, f, t * P:(t + 1) * P], w2[l][:, f, :], start=f == 0, stop=f == FC - 1)
                        mm.then_inc(filled[l], 1)

        @block.vector
        def _(dve):
            seconds, angle = emb[:, 0, 1, :], emb[:, 1, 0, :]
            turns, reduced, sin_cos, exp_neg, denom, silu = (emb[:, i, :, :] for i in range(2, 8))
            n = 0

            def link(ins):
                nonlocal n
                n += 1
                ins.then_inc(embed, 1)
                dve.wait_ge(embed, n)

            dve.wait_ge(ada_w_in, 64)
            link(dve.tensor_copy(emb[:, 0, 0, :], step_i[:, :]))
            link(dve.tensor_scalar(seconds, emb[:, 0, 0, :], RESCALE / NUM_STEPS, None, ALU.mult))
            link(dve.tensor_scalar(angle, seconds, freq[:, 0:1], None, ALU.mult))
            for i, offset in enumerate((0.0, 0.25)):
                link(dve.tensor_scalar(turns[:, i, :], angle, float(1 / (2 * np.pi)), offset, ALU.mult, ALU.add))
            link(dve.tensor_scalar(turns, turns, ROUND, None, ALU.add))
            link(dve.tensor_scalar(turns, turns, -ROUND, None, ALU.add))
            for k, part_of_turn in enumerate((TWO_PI_HI, TWO_PI_MID, TWO_PI_LO)):
                for i in range(2):
                    link(dve.scalar_tensor_tensor(out=reduced[:, i, :], in0=turns[:, i, :], scalar=-part_of_turn,
                                                  in1=reduced[:, i, :] if k else angle, op0=ALU.mult, op1=ALU.add))
            link(dve.tensor_scalar(reduced[:, 1, :], reduced[:, 1, :], float(np.pi / 2), None, ALU.add))
            link(dve.tensor_scalar(reduced, reduced, PI_IN, -PI_IN, ALU.min, ALU.max))
            assert n == N_EMBED
            dve.wait_ge(embed_act, 2)
            link(dve.tensor_scalar(denom, exp_neg, 1.0, None, ALU.add))
            link(dve.reciprocal(denom, denom))
            link(dve.tensor_tensor(silu, sin_cos, denom, ALU.mult))
            for c in range(C):
                for b in range(B):
                    last = dve.tensor_copy(act_bc[:, c, b, :], silu[:, c, b:b + 1].to_broadcast([P, P]))
            last.then_inc(ada_ready, 1)
            dve.wait_ge(consts_in, N_C)
            for l in range(2):
                dve.tensor_scalar(bqk[l][:, 0, :], bqk[l][:, 0, :], QSCALE, None, ALU.mult).then_inc(small_ready, 1)
            dve.tensor_scalar(b1k[:, :], b1[0][:, :], GELU_K, None, ALU.mult).then_inc(small_ready, 1)
            dve.memset(k6[ROWS:SHIFT, :, :], 1.0).then_inc(small_ready, 1)
            dve.memset(vx[:, :, :, :], 1.0).then_inc(small_ready, 1)
            for b in range(B):
                dve.wait_ge(ada_filled, b + 1)
                dve.tensor_tensor(ada[:, b, :], psS[:, b % 2, :], bada, ALU.add).then_inc(ada_ready, 1)
                dve.wait_ge(ada_ready, b + 2)
                dve.tensor_scalar(ada[:, b, 0:D], ada[:, b, 0:D], 1.0, None, ALU.add).then_inc(small_ready, 1)
            dve.wait_ge(small_ready, N_SMALL)

            measured_target = [Target(dve, measured[l], 1, 1) for l in range(2)]
            scores_target = Target(dve, s_filled[0], 1, 1)
            steps = [0, 0]

            def step(l, ins):
                steps[l] += 1
                ins.then_inc(v_step[l], 1)

            def stepped(l, b):
                dve.wait_ge(v_step[l], b * V_STEPS[l] + steps[l])

            def own_drained(l, b, d):
                dve.wait_ge(drained_v[l], FREE + b * DRAINS[l]["v"] + drains(l, d))

            def add_residual(l, b, d, dst, t):
                dve.wait_ge(filled[l], b * FILLS + d + 1)
                dve.tensor_tensor(dst, psT[:, d % 4, 0:D], resb[:, t, :], ALU.add).then_inc(drained_v[l], 1)

            def normalise(l, b, which):
                src = x1 if which else xl1 if l else xin
                adaptive = l == 0 and which == 0
                base = b * 2 * T + which * T
                if which:
                    dve.wait_ge(res_ready[l], b * (8 + 4 * l) + T)
                elif l:
                    dve.wait_ge(res_ready[0], (b + 1) * 8)
                else:
                    dve.wait_ge(x_in, b * 16 + 16)
                    dve.wait_ge(y_out, FREE + b * 16)
                for i in range(T + 3):
                    t = i
                    if t < T:
                        if which:
                            add_residual(l, b, OO + t, x1[:, t, :], t)
                            own_drained(l, b, OO + t)
                        elif l:
                            add_residual(0, b, F2 + t, xl1[:, t, :], t)
                            own_drained(0, b, F2 + t)
                        dve.bn_stats(stats[:, t, :], src[:, t, :]).then_inc(measured[l], 1)
                    t = i - 1
                    if 0 <= t < T:
                        measured_target[l].wait()
                        step(l, dve.bn_aggr(mv[:, t, :], stats[:, t, :]))
                        stepped(l, b)
                        dve.tensor_scalar(var_eps[:, t:t + 1], mv[:, t, 1:2], EPS, None, ALU.add).then_inc(stats_ready[l], 1)
                    t = i - 2
                    if 0 <= t < T:
                        dve.wait_ge(rstd_ready[l], base + t + 1)
                        if adaptive:
                            ins = dve.scalar_tensor_tensor(out=xr[:, t, :], in0=xin[:, t, :], scalar=mv[:, t, 0:1],
                                                           in1=ada[:, b, 0:D], op0=ALU.subtract, op1=ALU.mult)
                            if t < T - 1:
                                step(0, ins)
                                scaled = steps[0]
                            else:
                                ins.then_inc(xin_used, 1)
                        else:
                            dve.tensor_scalar(xh[:, t, :], src[:, t, :], mv[:, t, 0:1], rstd[:, t:t + 1], ALU.subtract, ALU.mult)\
                                .then_inc(norm_ready[l], 1)
                    t = i - 2
                    if adaptive and 0 <= t < T:
                        if t < T - 1:
                            dve.wait_ge(v_step[0], b * V_STEPS[0] + scaled)
                        else:
                            dve.wait_ge(xin_used, FREE + b + 1)
                        dve.scalar_tensor_tensor(out=xr[:, t, :], in0=xr[:, t, :], scalar=rstd[:, t:t + 1], in1=ada[:, b, D:2 * D],
                                                 op0=ALU.mult, op1=ALU.add).then_inc(norm_ready[0], 1)

            def turn_mask(b):
                low, inf, nan = (mask_row[:, i, :] for i in range(3))
                dve.wait_ge(mask_in, b * 16 + 16)
                dve.wait_ge(bias_masked, FREE + b * H)
                step(0, dve.tensor_scalar(mask_neg[:, :, :], mask_u8[:, :, :], -BIG, None, ALU.mult))
                stepped(0, b)
                step(0, dve.tensor_reduce(low, mask_neg[:, :, :], AX_X, ALU.max))
                stepped(0, b)
                step(0, dve.tensor_scalar(inf, low, 1e30, None, ALU.mult))
                stepped(0, b)
                step(0, dve.tensor_tensor(nan, inf, inf, ALU.subtract))
                stepped(0, b)
                for t in range(T):
                    last = dve.tensor_scalar(mask_neg[:, t, :], mask_neg[:, t, :], nan[:, t:t + 1], None, ALU.add)
                last.then_inc(mask_ready, 1)

            def split(l, b, c):
                dve.wait_ge(drained_a[l], b * DRAINS[l]["a"] + drains(l, QK + 2 * c + 1))
                full, left = qkf[:, :, c, :], rem[:, :, c, :]
                high, middle, low = (part[:, :, w, c, :] for w in range(PARTS))
                step(l, dve.tensor_copy(high, full))
                stepped(l, b)
                step(l, dve.tensor_tensor(left, full, high, ALU.subtract))
                stepped(l, b)
                step(l, dve.tensor_copy(middle, left))
                stepped(l, b)
                dve.tensor_tensor(low, left, middle, ALU.subtract).then_inc(parts_ready[l], 1)

            def keep_values(l, b, t):
                dve.wait_ge(filled[l], b * FILLS + VV + t + 1)
                dve.tensor_tensor(vx[:, t, :, 0:DH], psT[:, (VV + t) % 4, 0:D].rearrange("p (h d) -> p h d", d=DH),
                                  bv_all[l][:, :].rearrange("p (h d) -> p h d", d=DH), ALU.add).then_inc(drained_v[l], 1)

            def add_bias(b, h, t):
                i = h * T + t
                if t == 0:
                    dve.wait_ge(bias_masked, FREE + b * H + h + 1)
                scores_target.wait()
                dve.tensor_tensor_reduce(bias[:, h % G, t, :], s_banks[0][i % 2], bias[:, h % G, t, :], 1.0, -3e38,
                                         ALU.add, ALU.max, rmax[:, h, t:t + 1]).then_inc(s_drained[0], 1)

            def from_max(b, h, t):
                i = h * T + t
                dve.wait_ge(s_drained[0], FREE + b * H * T + i + 1)
                dve.tensor_scalar(bias[:, h % G, t, :], bias[:, h % G, t, :], rmax[:, h, t:t + 1], -1.0, ALU.subtract, ALU.mult)\
                    .then_inc(subbed_v, 1)

            def find_max(b, h, t):
                i = h * T + t
                dve.wait_ge(s_filled[1], b * H * T + i + 1)
                dve.tensor_reduce(rmax[:, h, t:t + 1], s_banks[1][i % 3][:, 0:width(t)], AX_X, ALU.max).then_inc(s_drained[1], 1)

            def split_max(b, g):
                m = rmax[:, g * G:(g + 1) * G, :].rearrange("p h t -> p (h t)")
                high, middle, low = (mparts[:, g % 2, w, :] for w in range(PARTS))
                left = rneg[:, g % 2, 0, :]
                dve.wait_ge(s_drained[1], FREE + b * H * T + G * T * (g + 1))
                dve.wait_ge(m_filled, FREE + b * NG + max(g - 1, 0))
                step(1, dve.tensor_scalar(high, m, -1.0, None, ALU.mult))
                stepped(1, b)
                step(1, dve.scalar_tensor_tensor(out=left, in0=m, scalar=-1.0, in1=high, op0=ALU.mult, op1=ALU.subtract))
                stepped(1, b)
                step(1, dve.tensor_copy(middle, left))
                stepped(1, b)
                dve.tensor_tensor(low, left, middle, ALU.subtract).then_inc(mparts_ready, 1)

            def divide_by_sums(l, b, g):
                rows = psM[:, :].rearrange("p (t j e) -> p t j e", t=T, e=QW)
                dve.wait_ge(raw_turned[l], b * NG + g + 1)
                step(l, dve.reciprocal(inv_sum[:, :, :], rows[:, :, :, DH]))
                stepped(l, b)
                dst = ctxn[:, :, g * G * DH:(g + 1) * G * DH].rearrange("p t (j d) -> p t j d", d=DH)
                dve.tensor_tensor(dst, rows[:, :, :, 0:DH], inv_sum[:, :, :].unsqueeze(3).to_broadcast([P, T, G, DH]), ALU.mult)\
                    .then_inc(ctx_normed[l], 1)

            with dve.Fori(0, B) as b:
                for l in range(2):
                    normalise(l, b, 0)
                    if l == 0:
                        turn_mask(b)
                    for c in range(C):
                        split(l, b, c)
                    for t in range(T):
                        keep_values(l, b, t)
                    if l == 0:
                        for h in range(H):
                            for t in range(T):
                                add_bias(b, h, t)
                                if t - 1 in V_TILES:
                                    from_max(b, h, t - 1)
                            if T - 1 in V_TILES:
                                from_max(b, h, T - 1)
                            if h % G == 2 and h > G:
                                divide_by_sums(0, b, h // G - 1)
                    else:
                        for g in range(NG + 1):
                            if g < NG:
                                for h in range(g * G, (g + 1) * G):
                                    for t in range(T):
                                        find_max(b, h, t)
                                split_max(b, g)
                            if g >= 3:
                                divide_by_sums(1, b, g - 3)
                        divide_by_sums(1, b, NG - 2)
                    divide_by_sums(l, b, NG - 1)
                    normalise(l, b, 1)
                    if l == 0:
                        for f in range(FC):
                            dve.wait_ge(sig_ready, b * FC + f + 1)
                            dve.scalar_tensor_tensor(out=gT[:, f, :], in0=psT[:, (F1 + f) % 4, :], scalar=b1[0][:, f:f + 1],
                                                     in1=sig[:, f % 2, :], op0=ALU.add, op1=ALU.mult).then_inc(drained_v[0], 1)
                dve.wait_ge(res_ready[1], (b + 1) * 12)
                for t in range(T):
                    add_residual(1, b, F2 + t, yout[:, t, :], t)
                for t in range(T):
                    own_drained(1, b, F2 + t)
                    dve.scalar_tensor_tensor(out=yout[:, t, :], in0=yout[:, t, :], scalar=gate[:, b, :], in1=xl1[:, t, :],
                                             op0=ALU.mult, op1=ALU.add).then_inc(y_ready, 1)
            assert steps == V_STEPS, steps


_NAMES = ("x itok_B_34_63 fside_Bx16xSxS_0 condB_gatescore mask_Bx1xSxS_bk0 "
          "L0_cond_W_ada L0_cond_b_ada L0_cond_Wq L0_cond_bq L0_cond_Wk L0_cond_bk L0_cond_Wv L0_cond_bv L0_cond_Wo L0_cond_bo "
          "L0_cond_W1 L0_cond_b1 L0_cond_W2 L0_cond_b2 L0_cond_g2 L0_cond_beta2 "
          "L1_cond_Wq L1_cond_bq L1_cond_Wk L1_cond_bk L1_cond_Wv L1_cond_bv L1_cond_Wo L1_cond_bo "
          "L1_cond_W1 L1_cond_b1 L1_cond_W2 L1_cond_b2 L1_cond_gamma1 L1_cond_beta1 L1_cond_gamma2 L1_cond_beta2").split()


def kernel(**inputs):
    import numpy as _np
    import concourse.bacc as _bacc
    from concourse import mybir as _mybir
    from concourse.bass_utils import run_bass_kernel_spmd as _run

    nc = _bacc.Bacc("TRN2", target_bir_lowering=False, num_devices=1)
    arrays, args = {}, {}
    for name in _NAMES:
        v = _np.ascontiguousarray(inputs[name])
        arrays[f"in_{name}"] = v
        args[name] = nc.dram_tensor(f"in_{name}", v.shape, _mybir.dt.from_np(v.dtype), kind="ExternalInput").ap()
    out = nc.dram_tensor("out", (B, S, D), F32, kind="ExternalOutput").ap()
    two_layers(nc, args, out)
    r = _run(nc, [arrays], core_ids=[0])
    return r.results[0]["out"]
```

```python
from contextlib import ExitStack

import numpy as np

import concourse.bass as bass
from concourse import mybir

F32 = mybir.dt.float32
BF16 = mybir.dt.bfloat16
U8 = mybir.dt.uint8
I32 = mybir.dt.int32
ALU = mybir.AluOpType
ACT = mybir.ActivationFunctionType
AX_X = mybir.AxisListType.X

P = 128
B, S, D = 4, 512, 256
H, DH, F = 16, 16, 1024
T = S // P
C = D // P
FC = F // P
G = 4
NG = H // G
QW = 32
PARTS = 3
Q_ROLE = [0, 0, 1, 0, 2, 1]
K_ROLE = [0, 1, 0, 2, 0, 1]
ROWS = DH * len(Q_ROLE)
SHIFT = ROWS + PARTS
QSCALE = DH ** -0.5
EPS = 1e-5
BIG = 1e37
GELU_K = 1.702
NUM_STEPS, RESCALE = 100.0, 4000.0
ROUND = 12582912.0
TWO_PI_HI, TWO_PI_MID = 6.28125, 0.0019350051879882812
TWO_PI_LO = float(2 * np.pi - TWO_PI_HI - TWO_PI_MID)
PI_IN = 3.1415925

ROLES_IN = 16 * 2 * len(Q_ROLE)
FREE = T

T1, QK, VV, OO, T2, F1, F2 = 0, 2, 6, 10, 14, 16, 24
FILLS = 28


def scored(h, t):
    ahead = t if h % G == 1 and h > G else max(t - 1, 0)
    return min(max(h * T + 2 + ahead, G * T), H * T)


def width(t):
    return (t + 1) * P


LEAD = 2 * G + 2
TWO_SETS = H - LEAD + 1
MAX_STEPS = (3, 6)
SLOTS = [G, G + 2]


def pool_tiles(h):
    return T if h < G else T - 1


def masked_by_pool(h):
    return sum(pool_tiles(i) for i in range(h))


def act_tiles(h):
    return range(T) if h < G else (1, 3)


def act_tiles_up_to(h):
    return sum(len(act_tiles(i)) for i in range(h + 1))


def drainer(layer, d):
    if d < VV or T2 <= d < F1:
        return "a"
    if F1 <= d < F2:
        return "a" if layer else "v"
    return "v"


def drains(layer, d):
    return sum(drainer(layer, e) == drainer(layer, d) for e in range(d + 1))


DRAINS = [{e: sum(drainer(l, d) == e for d in range(FILLS)) for e in "av"} for l in range(2)]
M_USES = [[("raw", 0), ("raw", 1), ("channels", 0), ("raw", 2), ("raw", 3), ("channels", 1)],
          [("max", 0), ("max", 1), ("max", 2), ("max", 3), ("raw", 0), ("raw", 1), ("channels", 0), ("raw", 2),
           ("raw", 3), ("channels", 1)]]
V_STEPS = [25, 30]


def two_layers(nc, a, out):
    freqs = np.exp(np.arange(P, dtype=np.float32) * np.float32(-np.log(10000.0) / (P - 1)))
    freq_table = nc.inline_tensor(freqs.astype(np.float32).reshape(P, 1))
    freq_dram = freq_table.ap()
    part_dram = nc.dram_tensor("part_dram", (2, PARTS, D, S), BF16, kind="Internal").ap()
    max_dram = nc.dram_tensor("max_dram", (NG, PARTS * G * T, P), BF16, kind="Internal").ap()
    bias_dram = a["fside_Bx16xSxS_0"].rearrange("b h (t p) k -> (b h) p t k", p=P)
    x_dram = a["x"].rearrange("b (t p) d -> b p t d", p=P)
    out_dram = out.rearrange("b (t p) d -> b p t d", p=P)
    mask_dram = a["mask_Bx1xSxS_bk0"].rearrange("b o (t p) k -> (b o) p t k", p=P)
    par = [{k.removeprefix(f"L{l}_cond_"): v for k, v in a.items() if k.startswith(f"L{l}_")} for l in range(2)]
    gam = [par[0]["g2"], par[1]["gamma2"]]
    bet = [par[0]["beta2"], par[1]["beta2"]]

    nc.disable_value_cache = True

    with ExitStack() as ctx:
        def sb(name, shape, dt=F32):
            return ctx.enter_context(nc.sbuf_tensor(name, shape, dt))

        def ps(name, shape, dt=F32):
            return ctx.enter_context(nc.psum_tensor(name, shape, dt))

        def sem(name):
            return ctx.enter_context(nc.semaphore(name))

        def sem2(name):
            return [sem(f"{name}{l}") for l in range(2)]

        wq, wk, wv, wo = ([sb(f"{n}{l}", [P, C, D]) for l in range(2)] for n in ("wq", "wk", "wv", "wo"))
        w1 = [sb(f"w1_{l}", [P, C, F]) for l in range(2)]
        w2 = [sb(f"w2_{l}", [P, FC, D]) for l in range(2)]
        bqk = [sb(f"bqk{l}", [P, 2, C]) for l in range(2)]
        b1 = [sb(f"b1_{l}", [P, FC]) for l in range(2)]
        b1k = sb("b1k", [P, FC])
        gb1 = sb("gb1", [P, 2, C])
        gb2 = [sb(f"gb2_{l}", [P, 2, C]) for l in range(2)]
        bv_all = [sb(f"bv_all{l}", [P, D]) for l in range(2)]
        bo_all = [sb(f"bo_all{l}", [P, D]) for l in range(2)]
        b2_all = [sb(f"b2_all{l}", [P, D]) for l in range(2)]
        gate = sb("gate", [P, B, 1])
        ada = sb("ada", [P, B, 2 * D])
        ident = sb("ident", [P, P])
        ident_b = sb("ident_b", [P, P], BF16)
        later_key = sb("later_key", [P, P], BF16)
        later_key_t = sb("later_key_t", [P, P], BF16)
        free = sb("free", [P, 32])
        freq = sb("freq", [P, 1])
        step_i = sb("step_i", [P, B], I32)
        emb = sb("emb", [P, 8, 2, B])
        mask_u8 = sb("mask_u8", [P, T, S], U8)
        mask_neg = sb("mask_neg", [P, T, S])
        mask_row = sb("mask_row", [P, 3, T])
        xin, xh, xr, resb, x1, xl1 = (sb(n, [P, T, D]) for n in ("xin", "xh", "xr", "resb", "x1", "xl1"))
        yout = resb
        stats = sb("stats", [P, T, 6])
        mv = sb("mv", [P, T, 2])
        var_eps, rstd, neg_half = (sb(n, [P, T]) for n in ("var_eps", "rstd", "neg_half"))
        hT = sb("hT", [P, C, S])
        q6 = sb("q6", [P, H, S], BF16)
        k6 = sb("k6", [P, H, S], BF16)
        vx = sb("vx", [P, T, H, QW])
        bias = sb("bias", [P, G, T, S])
        rmax = sb("rmax", [P, H, T])
        rneg = sb("rneg", [P, 2, G * T])
        mparts = sb("mparts", [P, 2, PARTS, G * T], BF16)
        mT = sb("mT", [PARTS * G * T, 2, P], BF16)
        craw = hT
        ctxn = x1
        ctxd = xh[:, :, :].rearrange("p (c a) n -> p c (a n)", c=C)
        inv_sum = sb("inv_sum", [P, T, G])
        work = sb("work", [P, G * T * S])
        prob = work[:, :].rearrange("p (g n) -> p g n", g=G)
        prob1 = work[:, 0:SLOTS[1] * 1280].rearrange("p (s n) -> p s n", n=1280)
        qkf = work[:, 0:2048].rearrange("p (x c n) -> p x c n", x=2, c=C)
        rem = work[:, 2048:4096].rearrange("p (x c n) -> p x c n", x=2, c=C)
        part = work[:, 4096:7168].bitcast(BF16).rearrange("p (x w c n) -> p x w c n", x=2, w=PARTS, c=C)
        gT = work[:, 0:4096].rearrange("p (f n) -> p f n", f=FC)
        sig = work[:, 4096:5120].rearrange("p (i n) -> p i n", i=2)
        wada = work[:, 0:1024].rearrange("p (c n) -> p c n", c=C)
        bada = work[:, 1024:1536]
        act_bc = work[:, 2048:3072].rearrange("p (c b n) -> p c b n", c=C, b=B)

        psS = ps("psS", [P, 2, S])
        psT = ps("psT", [P, 4, S])
        psC = ps("psC", [P, S])
        psM = ps("psM", [P, S])
        s_banks = [[psS[:, 0, :], psS[:, 1, :]], [psS[:, 0, :], psS[:, 1, :], psT[:, 3, :]]]

        def turned_halves(h):
            if h >= TWO_SETS and (h - TWO_SETS) % 2 == 0:
                return psS[:, :, :].rearrange("p a n -> p (a n)"), psT[:, 3, :]
            return psT[:, 0:2, :].rearrange("p a n -> p (a n)"), psT[:, 2, :]

        weights_in, ada_w_in, consts_in = sem("weights_in"), sem("ada_w_in"), sem("consts_in")
        made = sem("made")
        embed, embed_act, ada_filled, ada_ready = (sem(n) for n in ("embed", "embed_act", "ada_filled", "ada_ready"))
        small_ready = sem("small_ready")
        x_in, mask_in, mask_ready, xin_used = sem("x_in"), sem("mask_in"), sem("mask_ready"), sem("xin_used")
        bias_in = [sem(f"bias_in{s}") for s in range(G)]
        bias_masked, bias_masked_v, subbed_v, subbed_a = sem("bias_masked"), sem("bias_masked_v"), sem("subbed_v"), sem("subbed_a")
        v_step, measured = sem2("v_step"), sem2("measured")
        stats_ready, rstd_ready, norm_ready = sem2("stats_ready"), sem2("rstd_ready"), sem2("norm_ready")
        res_ready = sem2("res_ready")
        filled, drained_a, drained_v = sem2("filled"), sem2("drained_a"), sem2("drained_v")
        parts_ready, parts_out = sem2("parts_ready"), sem2("parts_out")
        roles_in = [[sem(f"roles_in{l}_{c}") for c in range(C)] for l in range(2)]
        s_filled, s_drained = sem2("s_filled"), sem2("s_drained")
        t_filled, exped = sem2("t_filled"), sem2("exped")
        pv_done = sem2("pv_done")
        raw_ready, raw_turned, ctx_normed = sem2("raw_ready"), sem2("raw_turned"), sem2("ctx_normed")
        ctx_turned, ctx_ready = sem2("ctx_turned"), sem2("ctx_ready")
        mparts_ready, m_filled, m_drained = sem("mparts_ready"), sem("m_filled"), sem("m_drained")
        m_out = sem("m_out")
        m_rows = [sem(f"m_rows{g}") for g in range(2)]
        sig_ready = sem("sig_ready")
        y_ready, y_out = sem("y_ready"), sem("y_out")

        N_W, N_C, N_MADE, N_EMBED, N_SMALL = 16 * 12, 16 * 19, 9, 15, 5 + B

        def wait_drained(eng, l, b, d):
            e = drainer(l, d)
            if e == "a":
                eng.wait_ge(drained_a[l], b * DRAINS[l][e] + drains(l, d))
            else:
                eng.wait_ge(drained_v[l], FREE + b * DRAINS[l][e] + drains(l, d))

        class Target:

            def __init__(self, eng, sem, first, step):
                self.eng, self.sem, self.step = eng, sem, step
                self.reg = eng.alloc_register()
                eng.reg_mov(self.reg, first)

            def wait(self, value):
                if isinstance(value, int):
                    self.eng.wait_ge(self.sem, value)
                else:
                    self.eng.wait_ge(self.sem, self.reg)
                    self.eng.reg_add(self.reg, self.reg, self.step)

        block = ctx.enter_context(nc.Block())

        @block.sync
        def _(sp):
            def col(v, n):
                return v.rearrange("(c p) -> p c", p=P)[:, 0:n]

            def row_all(v, n):
                return v.rearrange("(a n) -> a n", a=1).to_broadcast([P, n])

            def load_first():
                sp.dma_start(xin[:, :, :], x_dram[0]).then_inc(x_in, 16)
                sp.dma_start(mask_u8[:, :, :], mask_dram[0]).then_inc(mask_in, 16)

            load_first()
            sp.dma_start(wada, par[0]["W_ada"].rearrange("(c p) n -> p c n", p=P)).then_inc(ada_w_in, 16)
            sp.dma_start(bada, row_all(par[0]["b_ada"], 2 * D)).then_inc(ada_w_in, 16)
            sp.dma_start(step_i[:, :], a["itok_B_34_63"].rearrange("(a n) -> a n", a=1).to_broadcast([P, B])).then_inc(ada_w_in, 16)
            sp.dma_start(freq[:, :], freq_dram).then_inc(ada_w_in, 16)
            sp.dma_start(gate[:, :, 0], row_all(a["condB_gatescore"], B)).then_inc(consts_in, 16)
            n = 16
            for l in range(2):
                loads = [(bqk[l][:, 0, :], col(par[l]["bq"], C)), (bqk[l][:, 1, :], col(par[l]["bk"], C)),
                         (b1[l][:, :], col(par[l]["b1"], FC)), (gb2[l][:, 0, :], col(gam[l], C)),
                         (gb2[l][:, 1, :], col(bet[l], C)), (bv_all[l][:, :], row_all(par[l]["bv"], D)),
                         (bo_all[l][:, :], row_all(par[l]["bo"], D)), (b2_all[l][:, :], row_all(par[l]["b2"], D))]
                if l:
                    loads += [(gb1[:, 0, :], col(par[1]["gamma1"], C)), (gb1[:, 1, :], col(par[1]["beta1"], C))]
                for dst, src in loads:
                    with nc.allow_non_contiguous_dma(reason="per-channel columns, once"):
                        sp.dma_start(dst, src).then_inc(consts_in, 16)
                    n += 16
            assert n == N_C
            for h in range(2):
                sp.dma_start(bias[:, h, :, :], bias_dram[h]).then_inc(bias_in[h], 16)
            n = 0
            for l in range(2):
                for dst, name in ((wq, "Wq"), (wk, "Wk"), (wv, "Wv"), (wo, "Wo"), (w1, "W1"), (w2, "W2")):
                    sp.dma_start(dst[l][:, :, :], par[l][name].rearrange("(c p) n -> p c n", p=P)).then_inc(weights_in, 16)
                    n += 16
            assert n == N_W
            for h in range(2, G):
                sp.dma_start(bias[:, h, :, :], bias_dram[h]).then_inc(bias_in[h], 16)

            def to_roles(l, b):
                for c in range(C):
                    if l:
                        sp.wait_ge(roles_in[0][c], FREE + (b + 1) * ROLES_IN)
                        sp.wait_ge(pv_done[0], FREE + (b + 1) * NG * T)
                    else:
                        sp.wait_ge(roles_in[1][c], FREE + b * ROLES_IN)
                        sp.wait_ge(pv_done[1], FREE + b * NG * T)
                    sp.wait_ge(parts_ready[l], b * C + c + 1)
                    for x in range(2):
                        sp.dma_start(part_dram[x].rearrange("w (c p) n -> c p w n", p=P)[c], part[:, x, :, c, :]).then_inc(parts_out[l], 16)
                    sp.wait_ge(parts_out[l], b * 32 * C + 32 * (c + 1))
                    for x, (dst, roles) in enumerate(((q6, Q_ROLE), (k6, K_ROLE))):
                        for r, w in enumerate(roles):
                            sp.dma_start(dst[r * DH:(r + 1) * DH, c * H // C:(c + 1) * H // C, :],
                                         part_dram[x, w, c * P:(c + 1) * P].rearrange("(h d) n -> d h n", d=DH)).then_inc(roles_in[l][c], 16)

            def max_rows(b, g):
                sp.wait_ge(m_drained, FREE + b * NG + g + 1)
                sp.dma_start(max_dram[g], mT[:, g % 2, :]).then_inc(m_out, 16)
                sp.wait_ge(m_out, b * 16 * NG + 16 * (g + 1))
                sp.dma_start(q6[ROWS:SHIFT, g * G:(g + 1) * G, :].rearrange("p h (t k) -> p (h t) k", k=P),
                             max_dram[g].rearrange("(w r) k -> w r k", w=PARTS)).then_inc(m_rows[g % 2], 16)

            def load_bias(b, h):
                sp.dma_start(bias[:, h % G, :, :], bias_dram[b * H + h]).then_inc(bias_in[h % G], 16)

            def load_rows(b):
                sp.dma_start(xin[:, :, :], x_dram[b]).then_inc(x_in, 16)
                sp.dma_start(mask_u8[:, :, :], mask_dram[b]).then_inc(mask_in, 16)

            def reload(b, h):
                sp.wait_ge(t_filled[0], FREE + b * 2 * H + 2 * (h - G) + 2)
                load_bias(b, h)

            def batch(b, more):
                for h in range(G + 1, H):
                    reload(b, h)
                if more:
                    sp.wait_ge(mask_ready, FREE + b + 1)
                    load_rows(b + 1)
                to_roles(1, b)
                for g in range(NG):
                    max_rows(b, g)
                if more:
                    for h in range(G):
                        sp.wait_ge(t_filled[0], FREE + b * 2 * H + 2 * (H - G + h) + 2)
                        load_bias(b + 1, h)
                if more:
                    to_roles(0, b + 1)
                    reload(b + 1, G)
                sp.wait_ge(y_ready, b * T + T)
                sp.dma_start(out_dram[b], yout[:, :, :]).then_inc(y_out, 16)

            to_roles(0, 0)
            reload(0, G)
            with sp.Fori(0, B - 1) as b:
                batch(b, True)
            batch(B - 1, False)
            sp.wait_ge(y_out, FREE + 16 * B)

        @block.gpsimd
        def _(pool):
            from_free = [xin_used, mask_ready, m_drained, m_filled, y_out, bias_masked, *t_filled, *roles_in[0], *roles_in[1], *pv_done,
                         *drained_v, *s_drained, *raw_ready, *ctx_normed, *ctx_ready]
            for i, s in enumerate(from_free):
                pool.memset(free[:, i:i + 1], 0.0).then_inc(s, FREE)
            pool.memset(ident[:, :], 0.0).then_inc(made, 1)
            pool.memset(ident_b[:, :], 0.0).then_inc(made, 1)
            pool.memset(later_key[:, :], 0.0).then_inc(made, 1)
            pool.memset(later_key_t[:, :], 0.0).then_inc(made, 1)
            pool.memset(neg_half[:, :], -0.5).then_inc(made, 1)
            pool.wait_ge(made, 5)
            for m in (ident, ident_b):
                pool.affine_select(out=m[:, :], in_=m[:, :], compare_op=ALU.not_equal, fill=1.0, base=0,
                                   pattern=[[-1, P]], channel_multiplier=1).then_inc(made, 1)
            pool.affine_select(out=later_key[:, :], in_=later_key[:, :], compare_op=ALU.is_ge, fill=-BIG, base=0,
                               pattern=[[-1, P]], channel_multiplier=1).then_inc(made, 1)
            pool.affine_select(out=later_key_t[:, :], in_=later_key_t[:, :], compare_op=ALU.is_ge, fill=-BIG, base=0,
                               pattern=[[1, P]], channel_multiplier=-1).then_inc(made, 1)

            def inv_std(l, b, which):
                for t in range(T):
                    pool.wait_ge(stats_ready[l], b * 2 * T + which * T + t + 1)
                    pool.tensor_tensor(rstd[:, t:t + 1], var_eps[:, t:t + 1], neg_half[:, t:t + 1], ALU.pow).then_inc(rstd_ready[l], 1)

            def add_row(dst, src, row, ready):
                for t in range(T):
                    pool.tensor_tensor(dst[:, t, :], src[:, t, :], row[:, :], ALU.add).then_inc(ready, 1)

            def add_masks(b, heads):
                for h in heads:
                    if h == 0:
                        pool.wait_ge(mask_ready, FREE + b + 1)
                    pool.wait_ge(bias_in[h % G], b * 16 * NG + 16 * (h // G + 1))
                    for t in range(pool_tiles(h)):
                        pool.tensor_tensor(bias[:, h % G, t, :], bias[:, h % G, t, :], mask_neg[:, t, :], ALU.add).then_inc(bias_masked, 1)

            def start_batch(b):
                inv_std(0, b, 0)
                add_masks(b, range(G))

            def batch(b, more):
                for l in range(2):
                    if l:
                        inv_std(1, b, 0)
                    if l == 0:
                        add_masks(b, range(G, H))
                    if l:
                        pool.wait_ge(drained_v[0], FREE + (b + 1) * DRAINS[0]["v"])
                    else:
                        pool.wait_ge(norm_ready[0], b * 2 * T + T)
                        pool.wait_ge(y_out, FREE + b * 16)
                    add_row(resb, xl1 if l else xr, bo_all[l], res_ready[l])
                    if l and more:
                        start_batch(b + 1)
                    inv_std(l, b, 1)
                    per = 8 + 4 * l
                    add_row(resb, x1, b2_all[l], res_ready[l])
                    if l:
                        for t in range(T):
                            pool.wait_ge(res_ready[1], b * per + 5 + t)
                            pool.tensor_tensor(resb[:, t, :], resb[:, t, :], xl1[:, t, :], ALU.subtract).then_inc(res_ready[1], 1)

            pool.wait_ge(consts_in, N_C)
            start_batch(0)
            with pool.Fori(0, B - 1) as b:
                batch(b, True)
            batch(B - 1, False)

        @block.scalar
        def _(act):
            act.wait_ge(embed, N_EMBED)
            act.activation(emb[:, 4, :, :], emb[:, 3, :, :], ACT.Sin).then_inc(embed_act, 1)
            act.wait_ge(embed_act, 1)
            act.activation(emb[:, 5, :, :], emb[:, 4, :, :], ACT.Exp, scale=-1.0).then_inc(embed_act, 1)

            def out_of_bank(l, b, d, dst, scale, shift):
                act.wait_ge(filled[l], b * FILLS + d + 1)
                act.activation(dst, psT[:, d % 4, :], ACT.Identity, scale=scale, bias=shift).then_inc(drained_a[l], 1)

            def from_max(b, h, t):
                act.wait_ge(s_drained[0], FREE + b * H * T + h * T + t + 1)
                act.activation(bias[:, h % G, t, :], bias[:, h % G, t, :], ACT.Identity, scale=-1.0,
                               bias=rmax[:, h, t:t + 1]).then_inc(subbed_a, 1)

            def keep_context(l, b, g):
                act.wait_ge(pv_done[l], FREE + b * NG * T + T * (g + 1))
                if g >= 2:
                    act.wait_ge(raw_turned[l], b * NG + g - 1)
                act.activation(craw[:, g % 2, :], psC[:, :], ACT.Copy).then_inc(raw_ready[l], 1)

            def keep_channels(l, b, c):
                act.wait_ge(ctx_turned[l], b * C + c + 1)
                act.activation(ctxd[:, c, :], psM[:, :], ACT.Copy).then_inc(ctx_ready[l], 1)

            def exps(l, b, h, halves=(0, 1)):
                for p in halves:
                    j = 2 * h + p
                    act.wait_ge(t_filled[l], FREE + b * 2 * H + j + 1)
                    if h >= SLOTS[l]:
                        act.wait_ge(pv_done[l], FREE + b * NG * T + T * ((h - SLOTS[l]) // G) + 2 * p + 2)
                    if l:
                        lo, n = (0, 896) if p == 0 else (896, 384)
                        src, dst = turned_halves(h)[p][:, 0:n], prob1[:, h % SLOTS[1], lo:lo + n]
                    else:
                        src, dst = psT[:, 2 * p:2 * p + 2, :].rearrange("p a n -> p (a n)"), prob[:, h % G, p * 1024:(p + 1) * 1024]
                    act.activation(dst, src, ACT.Exp, scale=1.0 if l else -1.0).then_inc(exped[l], 1)

            def max_out(b, g):
                act.wait_ge(m_filled, FREE + b * NG + g + 1)
                if g >= 2:
                    act.wait_ge(m_out, b * 16 * NG + 16 * (g - 1))
                act.activation(mT[:, g % 2, :], psM[:, :].bitcast(BF16)[0:PARTS * G * T, 0:P], ACT.Copy).then_inc(m_drained, 1)

            def keep_turned(l, b):
                for c in range(C):
                    if l:
                        out_of_bank(l, b, T1 + c, hT[:, c, :], gb1[:, 0, c:c + 1], gb1[:, 1, c:c + 1])
                    else:
                        out_of_bank(l, b, T1 + c, hT[:, c, :], 1.0, 0.0)

            def keep_qk(l, b, chunks=range(C)):
                for c in chunks:
                    for x in range(2):
                        out_of_bank(l, b, QK + 2 * c + x, qkf[:, x, c, :], 1.0 if x else QSCALE, bqk[l][:, x, c:c + 1])

            def batch(b, more):
                for l in range(2):
                    if l:
                        keep_turned(1, b)
                        keep_qk(1, b)
                        max_out(b, 0)
                        max_out(b, 1)
                    act.wait_ge(parts_out[l], (b + 1) * 32 * C)
                    if l == 0:
                        for h in range(H + 1):
                            if G <= h < H:
                                for t in act_tiles(h)[:-1]:
                                    from_max(b, h, t)
                            if h:
                                exps(0, b, h - 1, (0,))
                            if h % G == 2 and h > 2:
                                keep_context(0, b, h // G - 1)
                            if G <= h < H:
                                from_max(b, h, act_tiles(h)[-1])
                            if h:
                                exps(0, b, h - 1, (1,))
                            if h == 3 * G + 1:
                                keep_channels(0, b, 0)
                        keep_context(0, b, NG - 1)
                    else:
                        for h in range(H):
                            exps(1, b, h)
                            if h in MAX_STEPS:
                                max_out(b, 2 + MAX_STEPS.index(h))
                            if h % G == 2 and h > 2:
                                keep_context(1, b, h // G - 1)
                            if h == 3 * G + 2:
                                keep_channels(1, b, 0)
                        keep_context(1, b, NG - 1)
                        if more:
                            act.wait_ge(raw_turned[1], (b + 1) * NG)
                            keep_turned(0, b + 1)
                            keep_qk(0, b + 1, (0,))
                    keep_channels(l, b, 1)
                    if l and more:
                        keep_qk(0, b + 1, (1,))
                    for c in range(C):
                        out_of_bank(l, b, T2 + c, hT[:, c, :], gb2[l][:, 0, c:c + 1], gb2[l][:, 1, c:c + 1])
                    if l and more:
                        act.wait_ge(parts_ready[0], (b + 2) * C)
                    for f in range(FC):
                        d = F1 + f
                        act.wait_ge(filled[l], b * FILLS + d + 1)
                        if l:
                            act.activation(gT[:, f, :], psT[:, d % 4, :], ACT.Gelu, bias=b1[1][:, f:f + 1]).then_inc(drained_a[1], 1)
                        else:
                            if f >= 2:
                                wait_drained(act, 0, b, d - 2)
                            act.activation(sig[:, f % 2, :], psT[:, d % 4, :], ACT.Sigmoid, scale=GELU_K,
                                           bias=b1k[:, f:f + 1]).then_inc(sig_ready, 1)
                if more:
                    for h in range(G):
                        for t in act_tiles(h):
                            from_max(b + 1, h, t)

            act.wait_ge(small_ready, N_SMALL)
            keep_turned(0, 0)
            keep_qk(0, 0)
            for h in range(G):
                for t in act_tiles(h):
                    from_max(0, h, t)
            with act.Fori(0, B - 1) as b:
                batch(b, True)
            batch(B - 1, False)

        @block.tensor
        def _(pe):
            mparts_target = Target(pe, mparts_ready, 1, 1)
            pe.wait_ge(ada_ready, 1)
            for b in range(B):
                if b >= 2:
                    pe.wait_ge(ada_ready, b)
                for c in range(C):
                    mm = pe.matmul(psS[:, b % 2, :], act_bc[:, c, b, :], wada[:, c, :], start=c == 0, stop=c == C - 1)
                mm.then_inc(ada_filled, 1)
            pe.wait_ge(weights_in, N_W)
            pe.wait_ge(made, N_MADE)
            pe.wait_ge(small_ready, N_SMALL)

            def bank(l, b, d, more=False):
                if more and l == 0:
                    wait_drained(pe, 1, b - 1, d + 4)
                elif more and OO <= d < F1 + 2:
                    wait_drained(pe, 0, b + 1, d - 8)
                elif d >= 4:
                    wait_drained(pe, l, b, d - 4)
                elif l:
                    pe.wait_ge(drained_v[0], FREE + (b + 1) * DRAINS[0]["v"])
                if l == 0 and OO <= d < T2:
                    pe.wait_ge(exped[0], (b + 1) * 2 * H)
                return psT[:, d % 4, :]

            def transposed(l, b, d, src, which, between=False):
                dst = [bank(l, b, d + c, between) for c in range(C)]
                for t in range(T):
                    pe.wait_ge(norm_ready[l], b * 2 * T + which * T + t + 1)
                    for c in range(C):
                        mm = pe.transpose(dst[c][:, t * P:(t + 1) * P], src[:, t, c * P:(c + 1) * P], ident[:, :])
                        if t == T - 1:
                            mm.then_inc(filled[l], 1)

            def scores(l, b, h, t):
                i = h * T + t
                banks = s_banks[l]
                if i >= len(banks):
                    pe.wait_ge(s_drained[l], FREE + b * H * T + i - len(banks) + 1)
                elif l:
                    pe.wait_ge(s_drained[0], FREE + (b + 1) * H * T)
                else:
                    pe.wait_ge(s_drained[1], FREE + b * H * T)
                n = width(t) if l else S
                dst = banks[i % len(banks)]
                mm = pe.matmul(dst[:, 0:n], q6[0:ROWS, h, t * P:(t + 1) * P], k6[0:ROWS, h, 0:n], start=True, stop=not l)
                if l:
                    mm = pe.matmul(dst[:, t * P:n], ident_b[:, :], later_key[:, :], start=False, stop=True)
                mm.then_inc(s_filled[l], 1)

            def half_free(l, b, h, p):
                if l and h == TWO_SETS:
                    pe.wait_ge(s_drained[1], FREE + (b + 1) * H * T)
                elif l and h > TWO_SETS:
                    pe.wait_ge(exped[l], b * 2 * H + 2 * (h - 2) + p + 1)
                elif h >= 1:
                    pe.wait_ge(exped[l], b * 2 * H + 2 * h + p - 1)

            def turn(b, h, kt):
                if h == 0:
                    pe.wait_ge(drained_v[1], FREE + b * DRAINS[1]["v"] - (T - 1 - kt))
                if kt == 0:
                    if h >= G:
                        pe.wait_ge(subbed_v, b * (H * T - act_tiles_up_to(H - 1)) + (h + 1) * T - act_tiles_up_to(h))
                    pe.wait_ge(subbed_a, b * act_tiles_up_to(H - 1) + act_tiles_up_to(h))
                if kt % 2 == 0:
                    half_free(0, b, h, kt // 2)
                for t in range(T):
                    mm = pe.transpose(psT[:, kt, t * P:(t + 1) * P], bias[:, h % G, t, kt * P:(kt + 1) * P], ident[:, :])
                if kt % 2:
                    mm.then_inc(t_filled[0], 1)

            def turned_scores(b, h, tiles):
                for kt in tiles:
                    n = S - kt * P
                    if kt % 2 == 0:
                        half_free(1, b, h, kt // 2)
                    lo = (0, 512, 0, 256)[kt]
                    dst = turned_halves(h)[kt // 2][:, lo:lo + n]
                    pe.matmul(dst, k6[0:SHIFT, h, kt * P:(kt + 1) * P], q6[0:SHIFT, h, kt * P:S], start=True, stop=False)
                    mm = pe.matmul(dst[:, 0:P], ident_b[:, :], later_key_t[:, :], start=False, stop=True)
                    if kt % 2:
                        mm.then_inc(t_filled[1], 1)

            def bank_m_free(l, b, use):
                kind, n = M_USES[l][use - 1] if use else M_USES[1 - l][-1]
                if use == 0:
                    l, b = 1 - l, (b if l else b - 1)
                if kind == "max":
                    pe.wait_ge(m_drained, FREE + b * NG + n + 1)
                elif kind == "raw":
                    pe.wait_ge(ctx_normed[l], FREE + b * NG + n + 1)
                else:
                    pe.wait_ge(ctx_ready[l], FREE + b * C + n + 1)

            def turn_context(l, b, g):
                bank_m_free(l, b, M_USES[l].index(("raw", g)))
                pe.wait_ge(raw_ready[l], FREE + b * NG + g + 1)
                for t in range(T):
                    mm = pe.transpose(psM[:, t * P:(t + 1) * P], craw[:, g % 2, t * P:(t + 1) * P], ident[:, :])
                mm.then_inc(raw_turned[l], 1)

            def turn_channels(l, b, c):
                bank_m_free(l, b, M_USES[l].index(("channels", c)))
                pe.wait_ge(ctx_normed[l], FREE + b * NG + 2 * c + 2)
                for t in range(T):
                    mm = pe.transpose(psM[:, t * P:(t + 1) * P], ctxn[:, t, c * P:(c + 1) * P], ident[:, :])
                mm.then_inc(ctx_turned[l], 1)

            def turn_max(b, g):
                bank_m_free(1, b, M_USES[1].index(("max", g)))
                mparts_target.wait(b * NG + g + 1)
                pe.transpose(psM[:, :].bitcast(BF16)[0:PARTS * G * T, 0:P], mparts[:, g % 2, :, :].rearrange("p w r -> p (w r)"), ident_b[:, :])\
                    .then_inc(m_filled, 1)

            def values(l, b, g, key_tiles=range(T)):
                if key_tiles[0] == 0:
                    if g:
                        pe.wait_ge(raw_ready[l], FREE + b * NG + g)
                    elif l:
                        pe.wait_ge(raw_ready[0], FREE + (b + 1) * NG)
                    else:
                        pe.wait_ge(raw_ready[1], FREE + b * NG)
                at = [0, 512, 896, 1152]
                for kt in key_tiles:
                    if kt % 2 == 0:
                        pe.wait_ge(exped[l], b * 2 * H + 2 * G * (g + 1) - 1 + kt // 2)
                    for j in range(G):
                        lo = kt * P if l else 0
                        rhs = prob1[:, (g * G + j) % SLOTS[1], at[kt]:at[kt] + S - lo] if l else prob[:, j, kt * S:(kt + 1) * S]
                        mm = pe.matmul(psC[j * QW:(j + 1) * QW, lo:S], vx[:, kt, g * G + j, :], rhs,
                                       start=kt == 0, stop=kt == T - 1)
                    mm.then_inc(pv_done[l], 1)

            def project_qk(l, b, chunks=range(C)):
                for n in chunks:
                    for x, w in enumerate((wq[l], wk[l])):
                        dst = bank(l, b, QK + 2 * n + x)
                        for c in range(C):
                            if x == 0 and n == 0:
                                wait_drained(pe, l, b, T1 + c)
                            mm = pe.matmul(dst, w[:, c, n * P:(n + 1) * P], hT[:, c, :], start=c == 0, stop=c == C - 1)
                        mm.then_inc(filled[l], 1)

            def project_v(l, b, between=False):
                for t in range(T):
                    dst = bank(l, b, VV + t, between)
                    for c in range(C):
                        mm = pe.matmul(dst[:, 0:D], hT[:, c, t * P:(t + 1) * P], wv[l][:, c, :], start=c == 0, stop=c == C - 1)
                    mm.then_inc(filled[l], 1)

            def output(l, b, c, more=False):
                pe.wait_ge(ctx_ready[l], FREE + b * C + c + 1)
                for t in range(T):
                    dst = psT[:, (OO + t) % 4, :] if c else bank(l, b, OO + t, more)
                    mm = pe.matmul(dst[:, 0:D], ctxd[:, c, t * P:(t + 1) * P], wo[l][:, c, :], start=c == 0, stop=c == C - 1)
                    if c == C - 1:
                        mm.then_inc(filled[l], 1)

            def batch(b, more):
                for l in range(2):
                    if l:
                        transposed(1, b, T1, xh, 0)
                        project_qk(1, b)
                        project_v(1, b)
                    wait_drained(pe, l, b, VV + T - 1)
                    if l == 0:
                        done = G * T
                        for h in range(H + 1):
                            if h == H // C:
                                pe.wait_ge(roles_in[0][1], FREE + (b + 1) * ROLES_IN)
                            for t in range(T):
                                due = scored(h, t)
                                for i in range(done, due):
                                    scores(0, b, i // T, i % T)
                                done = due
                                if h:
                                    turn(b, h - 1, t)
                                if h % G == 1 and h > 1:
                                    values(0, b, h // G - 1, (t,))
                                if h % G == 3 and h > 3 and t == 1:
                                    turn_context(0, b, h // G - 1)
                            if h == 3 * G:
                                turn_channels(0, b, 0)
                        values(0, b, NG - 1)
                    else:
                        for h in range(LEAD):
                            if h % (H // C) == 0:
                                pe.wait_ge(roles_in[1][h * C // H], FREE + (b + 1) * ROLES_IN)
                            for t in range(T):
                                scores(1, b, h, t)
                            if h == G + 1:
                                turn_max(b, 0)
                        turn_max(b, 1)
                        for h in range(H):
                            if h % G == 0:
                                pe.wait_ge(m_rows[h // G % 2], b * 32 + 16 * (h // G // 2 + 1))
                            for t, tiles in enumerate(((0,), (1,), (2, 3), ())):
                                turned_scores(b, h, tiles)
                                if LEAD + h < H:
                                    scores(1, b, LEAD + h, t)
                            if h in MAX_STEPS:
                                turn_max(b, 2 + MAX_STEPS.index(h))
                            if h % G == 1 and h > 1:
                                values(1, b, h // G - 1)
                            if h % G == 3 and h > 3:
                                turn_context(1, b, h // G - 1)
                            if h == 3 * G + 1:
                                turn_channels(1, b, 0)
                        values(1, b, NG - 1)
                        if more:
                            pe.wait_ge(exped[1], (b + 1) * 2 * H)
                            transposed(0, b + 1, T1, xr, 0)
                    if l == 0:
                        output(0, b, 0)
                    turn_context(l, b, NG - 1)
                    if l and more:
                        project_qk(0, b + 1, (0,))
                    turn_channels(l, b, 1)
                    if l and more:
                        project_qk(0, b + 1, (1,))
                    if l:
                        output(1, b, 0, more)
                    output(l, b, 1)
                    if l and more:
                        project_v(0, b + 1, True)
                    transposed(l, b, T2, xh, 1, l and more)
                    for f in range(FC):
                        dst = bank(l, b, F1 + f, l and more)
                        for c in range(C):
                            if f == 0:
                                wait_drained(pe, l, b, T2 + c)
                            mm = pe.matmul(dst, w1[l][:, c, f * P:(f + 1) * P], hT[:, c, :], start=c == 0, stop=c == C - 1)
                        mm.then_inc(filled[l], 1)
                    for t in range(T):
                        dst = bank(l, b, F2 + t)
                        if l and more and t == 0:
                            pe.wait_ge(roles_in[0][0], FREE + (b + 2) * ROLES_IN)
                        for f in range(FC):
                            if l and more and f % 2 == 1:
                                scores(0, b + 1, t, f // 2)
                            if t == 0:
                                wait_drained(pe, l, b, F1 + f)
                            mm = pe.matmul(dst[:, 0:D], gT[:, f, t * P:(t + 1) * P], w2[l][:, f, :], start=f == 0, stop=f == FC - 1)
                        mm.then_inc(filled[l], 1)

            transposed(0, 0, T1, xr, 0)
            project_qk(0, 0)
            project_v(0, 0)
            pe.wait_ge(roles_in[0][0], FREE + ROLES_IN)
            for h in range(G):
                for t in range(T):
                    scores(0, 0, h, t)
            with pe.Fori(0, B - 1) as b:
                batch(b, True)
            batch(B - 1, False)

        @block.vector
        def _(dve):
            seconds, angle = emb[:, 0, 1, :], emb[:, 1, 0, :]
            turns, reduced, sin_cos, exp_neg, denom, silu = (emb[:, i, :, :] for i in range(2, 8))
            n = 0

            def link(ins):
                nonlocal n
                n += 1
                ins.then_inc(embed, 1)
                dve.wait_ge(embed, n)

            dve.wait_ge(ada_w_in, 64)
            link(dve.tensor_copy(emb[:, 0, 0, :], step_i[:, :]))
            link(dve.tensor_scalar(seconds, emb[:, 0, 0, :], RESCALE / NUM_STEPS, None, ALU.mult))
            link(dve.tensor_scalar(angle, seconds, freq[:, 0:1], None, ALU.mult))
            for i, offset in enumerate((0.0, 0.25)):
                link(dve.tensor_scalar(turns[:, i, :], angle, float(1 / (2 * np.pi)), offset, ALU.mult, ALU.add))
            link(dve.tensor_scalar(turns, turns, ROUND, None, ALU.add))
            link(dve.tensor_scalar(turns, turns, -ROUND, None, ALU.add))
            for k, part_of_turn in enumerate((TWO_PI_HI, TWO_PI_MID, TWO_PI_LO)):
                for i in range(2):
                    link(dve.scalar_tensor_tensor(out=reduced[:, i, :], in0=turns[:, i, :], scalar=-part_of_turn,
                                                  in1=reduced[:, i, :] if k else angle, op0=ALU.mult, op1=ALU.add))
            link(dve.tensor_scalar(reduced[:, 1, :], reduced[:, 1, :], float(np.pi / 2), None, ALU.add))
            link(dve.tensor_scalar(reduced, reduced, PI_IN, -PI_IN, ALU.min, ALU.max))
            assert n == N_EMBED
            dve.wait_ge(embed_act, 2)
            link(dve.tensor_scalar(denom, exp_neg, 1.0, None, ALU.add))
            link(dve.reciprocal(denom, denom))
            link(dve.tensor_tensor(silu, sin_cos, denom, ALU.mult))
            for c in range(C):
                for b in range(B):
                    last = dve.tensor_copy(act_bc[:, c, b, :], silu[:, c, b:b + 1].to_broadcast([P, P]))
            last.then_inc(ada_ready, 1)
            dve.wait_ge(consts_in, N_C)
            for l in range(2):
                dve.tensor_scalar(bqk[l][:, 0, :], bqk[l][:, 0, :], QSCALE, None, ALU.mult).then_inc(small_ready, 1)
            dve.tensor_scalar(b1k[:, :], b1[0][:, :], GELU_K, None, ALU.mult).then_inc(small_ready, 1)
            dve.memset(k6[ROWS:SHIFT, :, :], 1.0).then_inc(small_ready, 1)
            dve.memset(vx[:, :, :, :], 1.0).then_inc(small_ready, 1)
            for b in range(B):
                dve.wait_ge(ada_filled, b + 1)
                slot = (b - 1) % B
                dve.tensor_tensor(ada[:, slot, :], psS[:, b % 2, :], bada, ALU.add).then_inc(ada_ready, 1)
                dve.wait_ge(ada_ready, b + 2)
                dve.tensor_scalar(ada[:, slot, 0:D], ada[:, slot, 0:D], 1.0, None, ALU.add).then_inc(small_ready, 1)
            dve.wait_ge(small_ready, N_SMALL)

            measured_target = [Target(dve, measured[l], first, 1) for l, first in enumerate((T + 1, 1))]
            scores_target = Target(dve, s_filled[0], G * T + 1, 1)
            steps = [0, 0]

            def step(l, ins):
                steps[l] += 1
                ins.then_inc(v_step[l], 1)

            def stepped(l, b):
                dve.wait_ge(v_step[l], b * V_STEPS[l] + steps[l])

            def own_drained(l, b, d):
                dve.wait_ge(drained_v[l], FREE + b * DRAINS[l]["v"] + drains(l, d))

            def add_residual(l, b, d, dst, t):
                dve.wait_ge(filled[l], b * FILLS + d + 1)
                dve.tensor_tensor(dst, psT[:, d % 4, 0:D], resb[:, t, :], ALU.add).then_inc(drained_v[l], 1)

            def normalise(l, b, which, slot=0, keep_next=False):
                src = x1 if which else xl1 if l else xin
                adaptive = l == 0 and which == 0
                base = b * 2 * T + which * T
                if which:
                    dve.wait_ge(res_ready[l], b * (8 + 4 * l) + T)
                elif l:
                    dve.wait_ge(res_ready[0], (b + 1) * 8)
                else:
                    dve.wait_ge(x_in, b * 16 + 16)
                for i in range(T + 3):
                    t = i
                    if keep_next and t >= T - 1:
                        keep_values(0, b + 1, t - T + 1)
                    if t < T:
                        if which:
                            add_residual(l, b, OO + t, x1[:, t, :], t)
                            own_drained(l, b, OO + t)
                        elif l:
                            add_residual(0, b, F2 + t, xl1[:, t, :], t)
                            own_drained(0, b, F2 + t)
                        dve.bn_stats(stats[:, t, :], src[:, t, :]).then_inc(measured[l], 1)
                    t = i - 1
                    if 0 <= t < T:
                        measured_target[l].wait(base + t + 1)
                        step(l, dve.bn_aggr(mv[:, t, :], stats[:, t, :]))
                        stepped(l, b)
                        dve.tensor_scalar(var_eps[:, t:t + 1], mv[:, t, 1:2], EPS, None, ALU.add).then_inc(stats_ready[l], 1)
                    t = i - 2
                    if 0 <= t < T:
                        dve.wait_ge(rstd_ready[l], base + t + 1)
                        if adaptive:
                            ins = dve.scalar_tensor_tensor(out=xr[:, t, :], in0=xin[:, t, :], scalar=mv[:, t, 0:1],
                                                           in1=ada[:, slot, 0:D], op0=ALU.subtract, op1=ALU.mult)
                            if t < T - 1:
                                step(0, ins)
                                scaled = steps[0]
                            else:
                                ins.then_inc(xin_used, 1)
                        else:
                            dve.tensor_scalar(xh[:, t, :], src[:, t, :], mv[:, t, 0:1], rstd[:, t:t + 1], ALU.subtract, ALU.mult)\
                                .then_inc(norm_ready[l], 1)
                    t = i - 2
                    if adaptive and 0 <= t < T:
                        if t < T - 1:
                            dve.wait_ge(v_step[0], b * V_STEPS[0] + scaled)
                        else:
                            dve.wait_ge(xin_used, FREE + b + 1)
                        dve.scalar_tensor_tensor(out=xr[:, t, :], in0=xr[:, t, :], scalar=rstd[:, t:t + 1], in1=ada[:, slot, D:2 * D],
                                                 op0=ALU.mult, op1=ALU.add).then_inc(norm_ready[0], 1)

            def turn_mask(b):
                low, inf, nan = (mask_row[:, i, :] for i in range(3))
                dve.wait_ge(mask_in, b * 16 + 16)
                dve.wait_ge(bias_masked, FREE + b * masked_by_pool(H))
                step(0, dve.tensor_scalar(mask_neg[:, :, :], mask_u8[:, :, :], -BIG, None, ALU.mult))
                stepped(0, b)
                step(0, dve.tensor_reduce(low, mask_neg[:, :, :], AX_X, ALU.max))
                stepped(0, b)
                step(0, dve.tensor_scalar(inf, low, 1e30, None, ALU.mult))
                stepped(0, b)
                step(0, dve.tensor_tensor(nan, inf, inf, ALU.subtract))
                stepped(0, b)
                for t in range(T):
                    last = dve.tensor_scalar(mask_neg[:, t, :], mask_neg[:, t, :], nan[:, t:t + 1], None, ALU.add)
                last.then_inc(mask_ready, 1)

            def split(l, b, c):
                dve.wait_ge(drained_a[l], b * DRAINS[l]["a"] + drains(l, QK + 2 * c + 1))
                full, left = qkf[:, :, c, :], rem[:, :, c, :]
                high, middle, low = (part[:, :, w, c, :] for w in range(PARTS))
                step(l, dve.tensor_copy(high, full))
                stepped(l, b)
                step(l, dve.tensor_tensor(left, full, high, ALU.subtract))
                stepped(l, b)
                step(l, dve.tensor_copy(middle, left))
                stepped(l, b)
                dve.tensor_tensor(low, left, middle, ALU.subtract).then_inc(parts_ready[l], 1)

            def keep_values(l, b, t):
                dve.wait_ge(filled[l], b * FILLS + VV + t + 1)
                dve.tensor_tensor(vx[:, t, :, 0:DH], psT[:, (VV + t) % 4, 0:D].rearrange("p (h d) -> p h d", d=DH),
                                  bv_all[l][:, :].rearrange("p (h d) -> p h d", d=DH), ALU.add).then_inc(drained_v[l], 1)

            def add_bias(b, h, t):
                i = h * T + t
                scores_target.wait(b * H * T + i + 1)
                dve.tensor_tensor_reduce(bias[:, h % G, t, :], s_banks[0][i % 2], bias[:, h % G, t, :], 1.0, -3e38,
                                         ALU.add, ALU.max, rmax[:, h, t:t + 1]).then_inc(s_drained[0], 1)

            def from_max(b, h, t):
                i = h * T + t
                dve.wait_ge(s_drained[0], FREE + b * H * T + i + 1)
                dve.tensor_scalar(bias[:, h % G, t, :], bias[:, h % G, t, :], rmax[:, h, t:t + 1], -1.0, ALU.subtract, ALU.mult)\
                    .then_inc(subbed_v, 1)

            def head_scores(b, h):
                for t in range(pool_tiles(h), T):
                    dve.wait_ge(bias_in[h % G], b * 16 * NG + 16 * (h // G + 1))
                    dve.tensor_tensor(bias[:, h % G, t, :], bias[:, h % G, t, :], mask_neg[:, t, :], ALU.add).then_inc(bias_masked_v, 1)
                for t in range(T):
                    if t >= pool_tiles(h):
                        dve.wait_ge(bias_masked_v, b * (H - G) + h - G + 1)
                    elif h >= G:
                        dve.wait_ge(bias_masked, FREE + b * masked_by_pool(H) + masked_by_pool(h) + t + 1)
                    elif t == 0:
                        dve.wait_ge(bias_masked, FREE + b * masked_by_pool(H) + masked_by_pool(h + 1))
                    add_bias(b, h, t)
                    if t and t - 1 not in act_tiles(h):
                        from_max(b, h, t - 1)

            def find_max(b, h, t):
                i = h * T + t
                dve.wait_ge(s_filled[1], b * H * T + i + 1)
                dve.tensor_reduce(rmax[:, h, t:t + 1], s_banks[1][i % 3][:, 0:width(t)], AX_X, ALU.max).then_inc(s_drained[1], 1)

            def split_max(b, g):
                m = rmax[:, g * G:(g + 1) * G, :].rearrange("p h t -> p (h t)")
                high, middle, low = (mparts[:, g % 2, w, :] for w in range(PARTS))
                left = rneg[:, g % 2, :]
                dve.wait_ge(s_drained[1], FREE + b * H * T + G * T * (g + 1))
                dve.wait_ge(m_filled, FREE + b * NG + max(g - 1, 0))
                step(1, dve.tensor_scalar(high, m, -1.0, None, ALU.mult))
                stepped(1, b)
                step(1, dve.scalar_tensor_tensor(out=left, in0=m, scalar=-1.0, in1=high, op0=ALU.mult, op1=ALU.subtract))
                stepped(1, b)
                step(1, dve.tensor_copy(middle, left))
                stepped(1, b)
                dve.tensor_tensor(low, left, middle, ALU.subtract).then_inc(mparts_ready, 1)

            def divide_by_sums(l, b, g):
                rows = psM[:, :].rearrange("p (t j e) -> p t j e", t=T, e=QW)
                dve.wait_ge(raw_turned[l], b * NG + g + 1)
                step(l, dve.reciprocal(inv_sum[:, :, :], rows[:, :, :, DH]))
                stepped(l, b)
                dst = ctxn[:, :, g * G * DH:(g + 1) * G * DH].rearrange("p t (j d) -> p t j d", d=DH)
                dve.tensor_tensor(dst, rows[:, :, :, 0:DH], inv_sum[:, :, :].unsqueeze(3).to_broadcast([P, T, G, DH]), ALU.mult)\
                    .then_inc(ctx_normed[l], 1)

            def start_rows(b, slot):
                assert steps[0] in (0, V_STEPS[0])
                steps[0] = 0
                normalise(0, b, 0, slot)

            def batch(b, more):
                steps[1] = 0
                for l in range(2):
                    if l:
                        normalise(1, b, 0)
                        for c in range(C):
                            split(1, b, c)
                        for t in range(T):
                            keep_values(1, b, t)
                    if l == 0:
                        for h in range(G, H):
                            head_scores(b, h)
                            if h % G == 3 and h > G:
                                divide_by_sums(0, b, h // G - 1)
                    else:
                        for g in range(NG):
                            for h in range(g * G, (g + 1) * G):
                                for t in range(T):
                                    find_max(b, h, t)
                            split_max(b, g)
                        divide_by_sums(1, b, 0)
                        if more:
                            start_rows(b + 1, b)
                        divide_by_sums(1, b, 1)
                        if more:
                            turn_mask(b + 1)
                        divide_by_sums(1, b, NG - 2)
                    divide_by_sums(l, b, NG - 1)
                    if l and more:
                        split(0, b + 1, 0)
                    normalise(l, b, 1, keep_next=l and more)
                    if l and more:
                        split(0, b + 1, 1)
                    if l == 0:
                        for f in range(FC):
                            dve.wait_ge(sig_ready, b * FC + f + 1)
                            dve.scalar_tensor_tensor(out=gT[:, f, :], in0=psT[:, (F1 + f) % 4, :], scalar=b1[0][:, f:f + 1],
                                                     in1=sig[:, f % 2, :], op0=ALU.add, op1=ALU.mult).then_inc(drained_v[0], 1)
                dve.wait_ge(res_ready[1], (b + 1) * 12)
                for t in range(T):
                    if more:
                        head_scores(b + 1, t)
                    add_residual(1, b, F2 + t, yout[:, t, :], t)
                for t in range(T):
                    own_drained(1, b, F2 + t)
                    dve.scalar_tensor_tensor(out=yout[:, t, :], in0=yout[:, t, :], scalar=gate[:, b, :], in1=xl1[:, t, :],
                                             op0=ALU.mult, op1=ALU.add).then_inc(y_ready, 1)

            start_rows(0, B - 1)
            turn_mask(0)
            for c in range(C):
                split(0, 0, c)
            for t in range(T):
                keep_values(0, 0, t)
            for h in range(G):
                head_scores(0, h)
            with dve.Fori(0, B - 1) as b:
                batch(b, True)
            batch(B - 1, False)
            assert steps == V_STEPS, steps


_NAMES = ("x itok_B_34_63 fside_Bx16xSxS_0 condB_gatescore mask_Bx1xSxS_bk0 "
          "L0_cond_W_ada L0_cond_b_ada L0_cond_Wq L0_cond_bq L0_cond_Wk L0_cond_bk L0_cond_Wv L0_cond_bv L0_cond_Wo L0_cond_bo "
          "L0_cond_W1 L0_cond_b1 L0_cond_W2 L0_cond_b2 L0_cond_g2 L0_cond_beta2 "
          "L1_cond_Wq L1_cond_bq L1_cond_Wk L1_cond_bk L1_cond_Wv L1_cond_bv L1_cond_Wo L1_cond_bo "
          "L1_cond_W1 L1_cond_b1 L1_cond_W2 L1_cond_b2 L1_cond_gamma1 L1_cond_beta1 L1_cond_gamma2 L1_cond_beta2").split()


def kernel(**inputs):
    import numpy as _np
    import concourse.bacc as _bacc
    from concourse import mybir as _mybir
    from concourse.bass_utils import run_bass_kernel_spmd as _run

    nc = _bacc.Bacc("TRN2", target_bir_lowering=False, num_devices=1)
    arrays, args = {}, {}
    for name in _NAMES:
        v = _np.ascontiguousarray(inputs[name])
        arrays[f"in_{name}"] = v
        args[name] = nc.dram_tensor(f"in_{name}", v.shape, _mybir.dt.from_np(v.dtype), kind="ExternalInput").ap()
    out = nc.dram_tensor("out", (B, S, D), F32, kind="ExternalOutput").ap()
    two_layers(nc, args, out)
    r = _run(nc, [arrays], core_ids=[0])
    return r.results[0]["out"]
```
